# Optimizing a Trainium2 kernel written in Bass

```python
import numpy as np
import jax
import jax.numpy as jnp

def _softmax(x, axis=-1):
    return jax.nn.softmax(x, axis=axis)

def _gelu(x):
    return jax.nn.gelu(x, approximate=True)

def _silu(x):
    return jax.nn.silu(x)

def _sigmoid(x):
    return jax.nn.sigmoid(x)

def _layernorm(x, axis=-1, eps=1e-05):
    m = jnp.mean(x, axis=axis, keepdims=True)
    v = jnp.var(x, axis=axis, keepdims=True)
    return (x - m) / jnp.sqrt(v + eps)

def _scatter_add(tgt, idx, src, axis=0):
    return tgt.at[idx].add(src)

def _segment_sum(src, seg, n):
    return jax.ops.segment_sum(src, seg, n)
kernel_name = 'mk_cond_resid_d4_seqx_r8_1dbbbb'

def setup_inputs(seed: int=0):
    np.random.seed(seed)
    _w = jnp.asarray

    def _rec_inputs():
        import jax
        import jax.numpy as jnp
        _rk = jax.random.key(seed)
        x = -0.000125 + 0.9999 * jax.random.normal(jax.random.fold_in(_rk, 1), (8, 128, 512), jnp.float32)
        _lenS = 128 - jax.random.randint(jax.random.fold_in(_rk, 7), (8,), 0, max(1, 128 // 4) + 1, jnp.int32)
        _lenS2 = 128 - jax.random.randint(jax.random.fold_in(_rk, 8), (8,), 0, max(1, 128 // 4) + 1, jnp.int32)
        condB_codebook = -0.0625 + 0.715345 * jax.random.normal(jax.random.fold_in(_rk, 11), (8,), jnp.float32)
        itok_B_3_7 = jax.random.randint(jax.random.fold_in(_rk, 12), (8,), 3, 8, jnp.int32)
        itok_B_0_2 = jax.random.randint(jax.random.fold_in(_rk, 13), (8,), 0, 3, jnp.int32)
        itok_B_0_7 = jax.random.randint(jax.random.fold_in(_rk, 14), (8,), 0, 8, jnp.int32)
        return (x, condB_codebook, itok_B_3_7, itok_B_0_2, itok_B_0_7)
    x, condB_codebook, itok_B_3_7, itok_B_0_2, itok_B_0_7 = _rec_inputs()

    def _L0_cond_setup():
        import jax, jax.numpy as jnp
        import numpy as np
        GROUP = 128
        LORA_ALPHA = 32.0
        LORA_RANK = 64
        key = jax.random.key(seed)
        k1, k2, k3, k4 = jax.random.split(key, 4)
        O, I = (512, 512)
        x = jax.random.normal(k1, (4, 256, I), dtype=jnp.float32)
        weight = jax.random.normal(k2, (O, I), dtype=jnp.float32) * 0.02
        wg = weight.reshape(O, I // GROUP, GROUP)
        scale_log = jnp.log(jnp.clip(jnp.max(jnp.abs(wg), axis=2, keepdims=True), 1e-05))
        codebook = jnp.array([-1.0, -0.25, 0.0, 1.0], dtype=jnp.float32)
        lora_A = jax.random.normal(k3, (LORA_RANK, I), dtype=jnp.float32) * 0.02
        lora_B = jax.random.normal(k4, (O, LORA_RANK), dtype=jnp.float32) * 0.02
        return {'x': x, 'weight': weight, 'scale_log': scale_log, 'codebook': codebook, 'lora_A': lora_A, 'lora_B': lora_B}
    _L0_cond_all = _L0_cond_setup()
    _L0_cond_in = {k: v for k, v in _L0_cond_all.items() if k in ('weight', 'scale_log', 'lora_A', 'lora_B')}
    del _L0_cond_all

    def _L1_cond_setup():
        import jax, jax.numpy as jnp
        import numpy as np
        RANK = 16
        ALPHA = 16.0
        SCALING = ALPHA / RANK
        N_ADAPTERS = 8
        IN_F = 512
        OUT_F = 512
        BATCH = 4
        SEQ = 256
        key = jax.random.key(seed)
        kx, ka, kb, ki = jax.random.split(key, 4)
        x = jax.random.normal(kx, (BATCH, SEQ, IN_F), dtype=jnp.float32)
        A = jax.random.normal(ka, (N_ADAPTERS, OUT_F, RANK), dtype=jnp.float32) * 0.02
        B = jax.random.normal(kb, (N_ADAPTERS, RANK, IN_F), dtype=jnp.float32) * 0.02
        adapter_ids = jax.random.randint(ki, (BATCH,), 0, N_ADAPTERS, dtype=jnp.int32)
        return {'x': x, 'A': A, 'B': B, 'adapter_ids': adapter_ids}
    _L1_cond_all = _L1_cond_setup()
    _L1_cond_in = {k: v for k, v in _L1_cond_all.items() if k in ('A', 'B')}
    del _L1_cond_all

    def _L2_cond_setup():
        import jax, jax.numpy as jnp
        import numpy as np
        B, S, D_IN, D_OUT = (4, 256, 512, 512)
        R, NUM_LABELERS = (32, 5)
        LORA_SCALING = 16 / 32
        key = jax.random.key(seed)
        k1, k2, k3, k4, k5 = jax.random.split(key, 5)
        x = jax.random.normal(k1, (B, S, D_IN), dtype=jnp.float32)
        labeler_index = jax.random.randint(k2, (B,), 0, NUM_LABELERS, dtype=jnp.int64)
        W = jax.random.normal(k3, (D_OUT, D_IN), dtype=jnp.float32) * 0.02
        lora_A = jax.random.normal(k4, (NUM_LABELERS, D_IN, R), dtype=jnp.float32) * 0.02
        lora_B_w = jax.random.normal(k5, (D_OUT, R), dtype=jnp.float32) * 0.02
        return {'x': x, 'labeler_index': labeler_index, 'W': W, 'lora_A': lora_A, 'lora_B_w': lora_B_w}
    _L2_cond_all = _L2_cond_setup()
    _L2_cond_in = {k: v for k, v in _L2_cond_all.items() if k in ('W', 'lora_A', 'lora_B_w')}
    del _L2_cond_all

    def _L3_cond_setup():
        import jax, jax.numpy as jnp
        import numpy as np
        TOP_K = 2
        LANG_BIAS = 5.0
        SCALING = 32.0 / 16.0
        LANGUAGE_PAD_ID = -1
        key = jax.random.key(seed)
        ks = jax.random.split(key, 6)
        B, T, D, O, E, R = (4, 256, 512, 512, 8, 16)
        x = jax.random.normal(ks[0], (B, T, D), dtype=jnp.float32)
        language_ids = jax.random.randint(ks[1], (B,), 0, E).astype(jnp.int64)
        W = jax.random.normal(ks[2], (O, D), dtype=jnp.float32) * (1.0 / np.sqrt(D))
        Wr = jax.random.normal(ks[3], (E, D), dtype=jnp.float32) * (1.0 / np.sqrt(D))
        A = jax.random.normal(ks[4], (E, R, D), dtype=jnp.float32) * (1.0 / np.sqrt(D))
        Bm = jax.random.normal(ks[5], (O, R), dtype=jnp.float32) * 0.0
        Bm = jnp.broadcast_to(Bm, (E, O, R)) + jax.random.normal(ks[5], (E, O, R), dtype=jnp.float32) * 0.02
        return {'x': x, 'language_ids': language_ids, 'W': W, 'Wr': Wr, 'A': A, 'B': Bm}
    _L3_cond_all = _L3_cond_setup()
    _L3_cond_in = {k: v for k, v in _L3_cond_all.items() if k in ('W', 'Wr', 'A', 'B')}
    del _L3_cond_all
    return {'x': x, 'condB_codebook': condB_codebook, 'itok_B_3_7': itok_B_3_7, 'itok_B_0_2': itok_B_0_2, 'itok_B_0_7': itok_B_0_7, 'L0_cond_weight': _L0_cond_in['weight'], 'L0_cond_scale_log': _L0_cond_in['scale_log'], 'L0_cond_lora_A': _L0_cond_in['lora_A'], 'L0_cond_lora_B': _L0_cond_in['lora_B'], 'L1_cond_A': _L1_cond_in['A'], 'L1_cond_B': _L1_cond_in['B'], 'L2_cond_W': _L2_cond_in['W'], 'L2_cond_lora_A': _L2_cond_in['lora_A'], 'L2_cond_lora_B_w': _L2_cond_in['lora_B_w'], 'L3_cond_W': _L3_cond_in['W'], 'L3_cond_Wr': _L3_cond_in['Wr'], 'L3_cond_A': _L3_cond_in['A'], 'L3_cond_B': _L3_cond_in['B']}

def reference(x, condB_codebook, itok_B_3_7, itok_B_0_2, itok_B_0_7, L0_cond_weight, L0_cond_scale_log, L0_cond_lora_A, L0_cond_lora_B, L1_cond_A, L1_cond_B, L2_cond_W, L2_cond_lora_A, L2_cond_lora_B_w, L3_cond_W, L3_cond_Wr, L3_cond_A, L3_cond_B):
    import jax
    import jax.numpy as jnp

    def _L0_cond_ref(x, weight, scale_log, codebook, lora_A, lora_B):
        import jax, jax.numpy as jnp
        import numpy as np
        GROUP = 128
        LORA_ALPHA = 32.0
        LORA_RANK = 64
        O, I = weight.shape
        lora_delta = lora_B @ lora_A * (LORA_ALPHA / LORA_RANK)
        cb = codebook / jnp.clip(jnp.max(jnp.abs(codebook)), 1e-08)
        scale = jnp.exp(scale_log)
        wg = (weight + lora_delta).reshape(O, I // GROUP, GROUP)
        normalized = wg / scale
        thresholds = (cb[:-1] + cb[1:]) * 0.5
        idx = jnp.searchsorted(thresholds, normalized, side='left')
        quantized = cb[idx]
        w = jax.lax.stop_gradient(quantized - normalized) + normalized
        w_q = (w * scale).reshape(O, I)
        w_eff = w_q + lora_delta
        return x @ w_eff.T

    def _L1_cond_ref(x, A, B, adapter_ids):
        import jax, jax.numpy as jnp
        import numpy as np
        RANK = 16
        ALPHA = 16.0
        SCALING = ALPHA / RANK
        N_ADAPTERS = 8
        IN_F = 512
        OUT_F = 512
        BATCH = 4
        SEQ = 256
        B_sel = B[adapter_ids]
        A_sel = A[adapter_ids]
        Bx = jnp.einsum('bni,bri->bnr', x, B_sel)
        out = jnp.einsum('bnr,bor->bno', Bx, A_sel)
        return out * SCALING

    def _L2_cond_ref(x, labeler_index, W, lora_A, lora_B_w):
        import jax, jax.numpy as jnp
        import numpy as np
        B, S, D_IN, D_OUT = (4, 256, 512, 512)
        R, NUM_LABELERS = (32, 5)
        LORA_SCALING = 16 / 32
        base = jnp.einsum('bsi,oi->bso', x, W)
        labelers_A = lora_A[labeler_index]
        low = jnp.einsum('bsi,bir->bsr', x, labelers_A)
        delta = jnp.einsum('bsr,or->bso', low, lora_B_w) * LORA_SCALING
        return base + delta

    def _L3_cond_ref(x, language_ids, W, Wr, A, B):
        import jax, jax.numpy as jnp
        import numpy as np
        TOP_K = 2
        LANG_BIAS = 5.0
        SCALING = 32.0 / 16.0
        LANGUAGE_PAD_ID = -1
        base = jnp.einsum('btd,od->bto', x, W)
        E = Wr.shape[0]
        logits = jnp.einsum('btd,ed->bte', x.astype(jnp.float32), Wr.astype(jnp.float32))
        expert_targets = language_ids
        valid = expert_targets >= 0
        tgt = jnp.where(valid, expert_targets, 0)
        bias = jax.nn.one_hot(tgt, E, dtype=logits.dtype) * LANG_BIAS
        bias = jnp.where(valid[:, None], bias, 0.0)
        logits = logits + bias[:, None, :]
        topw, topi = jax.lax.top_k(logits, TOP_K)
        weights = jax.nn.softmax(topw, axis=-1)
        gates = jnp.sum(jax.nn.one_hot(topi, E, dtype=weights.dtype) * weights[..., None], axis=-2)
        gates = gates.astype(x.dtype)
        h = jnp.einsum('btd,erd->bter', x, A)
        lora_out = jnp.einsum('bter,bte,eor->bto', h, gates, B)
        return base + SCALING * lora_out
    x = x + _L0_cond_ref(x, L0_cond_weight, L0_cond_scale_log, condB_codebook, L0_cond_lora_A, L0_cond_lora_B)
    x = x + _L1_cond_ref(x, L1_cond_A, L1_cond_B, itok_B_3_7)
    x = x + _L2_cond_ref(x, itok_B_0_2, L2_cond_W, L2_cond_lora_A, L2_cond_lora_B_w)
    x = x + _L3_cond_ref(x, itok_B_0_7, L3_cond_W, L3_cond_Wr, L3_cond_A, L3_cond_B)
    return x

_drawn_inputs = setup_inputs


def setup_inputs(seed=0):
    import zlib

    import numpy as np

    out = dict(_drawn_inputs(seed))
    spreads = {}
    factors = {'L2_cond_lora_A': 2.829, 'L2_cond_lora_B_w': 2.823, 'L3_cond_Wr': 3.993}
    for name, (base, spread) in spreads.items():
        noise = np.random.default_rng([zlib.crc32(name.encode()), seed]).standard_normal(out[name].shape)
        drawn = base * np.exp(spread * noise) if base else spread * noise
        out[name] = jnp.asarray(drawn.astype(out[name].dtype))
    for name, factor in factors.items():
        out[name] = (out[name] * factor).astype(out[name].dtype)
    return out
```

```python
from contextlib import ExitStack

import concourse.bass as bass
from concourse import mybir

F32 = mybir.dt.float32
F32R = mybir.dt.float32r
I32 = mybir.dt.int32
U32 = mybir.dt.uint32
ALU = mybir.AluOpType
ACT = mybir.ActivationFunctionType
AX = mybir.AxisListType

P = 128
HI, LO = 0, 1
PASSES = ((HI, HI), (HI, LO), (LO, HI))


def layer_chain(nc, x, codebook, adapter_id, labeler_id, language_id, W0, scale_log, LA0, LB0, A1, B1, W2, L2, R2,
                W3, Wr, A3, B3, out):
    NB, T, D = x.shape
    KT = D // P
    G = KT
    RL0 = LA0.shape[0]
    RA = A1.shape[2]
    RB = L2.shape[2]
    E, RE = A3.shape[0], A3.shape[1]
    NC = E + E * RE
    V = RB + RA
    QW = D + NC
    RW = QW + NB * V
    QP = QW // 2
    RP = RW // 3
    BG = P // RB
    GW = BG * V
    SEG = (BG * RB + RA)
    XW = QW + D
    NCB = codebook.shape[0]
    assert (T, D, NC, V, RB * KT, NCB, E) == (P, 512, 136, 48, P, 8, 8) and RW % 3 == 0
    LORA0_SCALE, L2_SCALE, L3_SCALE, LANG_BIAS = 0.5, 0.5, 2.0, 5.0
    LO_ROW = 64
    VW = LO_ROW + V
    NS, NOUT = 3, 3
    WARM_UPS, WARM_AGAIN = 12, 7

    ctx = ExitStack()
    with ctx:
        at = [(nc.sbuf_base + 63) // 64 * 64]

        def put(name, shape, dt, offset):
            return nc.alloc_sbuf_tensor_at(name, shape, dt, offset=offset)

        def sb(name, shape, dt=F32):
            n = 4
            for s in shape[1:]:
                n *= s
            offset = at[0]
            at[0] += (n + 63) // 64 * 64
            assert at[0] <= nc.sbuf_top, (name, at[0], nc.sbuf_top)
            return put(name, shape, dt, offset), offset

        w0, w0_at = sb("w0", [P, KT, D])
        w2, w2_at = sb("w2", [P, KT, D])
        w3, w3_at = sb("w3", [P, KT, D])
        x_a, _ = sb("x_first_half", [P, NB // 2, D])
        x_b = put("x_second_half", [P, NB // 2, D], F32, w3_at)
        early_at = at[0]
        lb, _ = sb("lb", [P, KT, RL0])
        la, _ = sb("la", [RL0, D])
        la_s, _ = sb("la_split", [RL0, 2, D], F32R)
        lbt_s, _ = sb("lbt_split", [RL0, 2, D], F32R)
        a3, _ = sb("a3", [P, D])
        b1, _ = sb("b1", [P, D])
        l2, _ = sb("l2", [P, KT, NB, RB])
        early_end = at[0]
        r2, _ = sb("r2", [P, KT, RB])
        b3, _ = sb("b3", [P, KT, E, RE])
        xt, xt_at = sb("xt_split", [P, 2, NB, KT, T], F32R)
        kb = D * 4
        r2_x = put("r2_scaled", [P, KT, KT, RB], F32, xt_at)
        r2_s = put("r2_split", [P, 2, KT, P], F32R, xt_at + kb)
        a1 = put("a1", [P, KT, NB, RA], F32, xt_at + 3 * kb)
        a1_s = put("a1_split", [P, 2, KT, P], F32R, xt_at + 4 * kb)
        wr = put("wr", [E, D], F32, xt_at + 8 * kb)
        al_raw = put("al_raw", [P, 2, 2, P], F32, xt_at + 6 * kb)
        al_s = put("al_split", [P, 2, 2, P], F32R, xt_at + 7 * kb)
        w0_s, _ = sb("w0_split", [P, 2, KT, D], F32R)
        pc, _ = sb("p3c_w2_then_r", [P, 2, KT, XW], F32R)
        qc, _ = sb("qc_split", [P, 2, KT, RW], F32R)
        b3t, _ = sb("b3t_split", [P, 2, D], F32R)
        t1 = put("t1_split", [P, 2, QW], F32R, w2_at)
        t2, _ = sb("t2_split", [P, 2, QW], F32R)
        s_hi = put("s_hi", [VW, NS, QW], F32R, early_at)
        s_lo = put("s_lo", [V, NS, QW], F32R, early_at + NS * QW * 4)
        assert early_end - early_at >= 2 * NS * QW * 4, (early_end - early_at)
        outs = put("out_rows", [P, NOUT, D], F32, w0_at)
        ld, _ = sb("ld", [P, KT, D])
        nrm, _ = sb("normalized", [P, G, KT, P])
        acc, acc_at = sb("level_sum", [P, 2, KT, P])
        bia, _ = sb("level_biased", [P, 2, KT, P])
        ident, _ = sb("ident", [P, P])
        diag, _ = sb("diag", [P, 2, NB, RA])
        iota_i, _ = sb("iota_i", [P, E], I32)
        iota, _ = sb("iota", [P, E])
        ids_a, _ = sb("ids_adapter", [1, NB], I32)
        ids_l, _ = sb("ids_labeler", [1, NB], I32)
        lang_i, _ = sb("lang_i", [P, NB], I32)
        lang, _ = sb("lang", [P, NB])
        lbias, _ = sb("lang_bias", [P, NB, E])
        cb, _ = sb("cb", [P, NCB])
        cbn, _ = sb("cbn", [P, NCB])
        thr, _ = sb("thr", [P, NCB])
        step, _ = sb("step", [P, NCB])
        tiny, _ = sb("tiny", [P, 4])
        slog, _ = sb("slog", [P, KT, G])
        scale, _ = sb("scale", [P, KT, G])
        rscale, _ = sb("rscale", [P, KT, G])
        vn = put("v_rows", [P, 2, P], F32R, acc_at)
        vt = put("v_cols", [P, 2, T], F32R, acc_at + 2 * P * 4)
        lg, _ = sb("logits", [P, E])
        top, _ = sb("top", [P, 8])
        top_i, _ = sb("top_i", [P, 8], U32)
        top_f, _ = sb("top_f", [P, 8])
        gw, _ = sb("gate_weights", [P, 8])
        gate, _ = sb("gate", [P, 3, E])
        hg = put("h_gated", [P, 2, E * RE], F32, acc_at + 4 * P * 4)
        hgt = put("hgt_split", [P, 2, T], F32R, acc_at + 6 * P * 4)

        ps = ctx.enter_context(nc.psum_tensor("ps", [P, 8, 512], F32))

        def sem(name):
            return ctx.enter_context(nc.semaphore(name))

        ld_ids, ld_lang, ld_cb, ld_scale, ld_lb, ld_la = (
            sem(f"loaded_{n}") for n in ("ids", "lang", "cb", "scale", "lb", "la"))
        ld_w3 = [sem(f"loaded_w3_{i}") for i in range(2)]
        ld_w2 = [sem(f"loaded_w2_{i}") for i in range(2)]
        ld_w0 = [sem(f"loaded_w0_{i}") for i in range(2)]
        ld_wr, ld_a3, ld_b3, ld_r2, ld_b1, ld_l2, ld_a1 = (
            sem(f"loaded_{n}") for n in ("wr", "a3", "b3", "r2", "b1", "l2", "a1"))
        ld_x = [sem(f"loaded_x_{i}") for i in range(2)]
        s_loaded = [sem(f"s_loaded_{i}") for i in range(NS)]
        stored = [sem(f"stored_{i}") for i in range(NOUT)]
        made = sem("constants_made")
        s_zeroed = sem("s_rows_zeroed")
        eye3, eye2 = sem("w3_plus_identity"), sem("w2_plus_identity")
        shifted, eye_ld = sem("w0_plus_ld"), sem("ld_plus_identity")
        diag_made = sem("diag_made")
        w2_hi, w2_last_lo, w2_low = sem("w2_hi"), sem("w2_last_lo"), sem("w2_low")
        la_hi, la_lo = sem("la_hi"), sem("la_lo")
        a1_hi, a1_lo = sem("a1_hi"), sem("a1_lo")
        l2_hi, l2_lo = sem("l2_hi"), sem("l2_lo")
        r2_hi, r2_lo = sem("r2_hi"), sem("r2_lo")
        al_masked, al_split = sem("al_masked"), sem("al_split")
        filled, high, low = sem("bank_filled"), sem("bank_high"), sem("bank_low")
        exped, dve_chain = sem("scale_exp"), sem("dve_chain")
        rs_ready, q_n0 = sem("rscale_ready"), sem("quant_first_normal")
        q_n, q_sum, q_bias, q_err, q_fin = (sem(f"quant_{n}") for n in ("normal", "sum", "bias", "err", "fin"))
        w0_hi, w0_lo = sem("w0_hi"), sem("w0_lo")
        small_done, v_hi, v_lo, vt_up, vt_copied, z_small, z_main = (
            sem(n) for n in ("small_done", "v_hi", "v_lo", "v_turned", "v_copied", "z_small", "z_main"))
        gap_ready, exp_done, hg_ready, hgt_up, hgt_hi, hgt_lo, main_done, out_copied = (
            sem(n) for n in ("gap_ready", "exp_done", "hg_ready", "hg_turned", "hgt_hi", "hgt_lo", "main_done",
                             "out_copied"))

        USES = (["lbt"] + [f"ld{i}" for i in range(KT)] + [f"p3_{i}" for i in range(KT)] + ["c0", "c1", "t2a", "t2b"]
                + [f"qc{i}{h}" for i in range(KT - 1) for h in "ab"]
                + ["qc3a", "al", "qc3b", "b3t", "b1t", "t1a", "t1b"] + [f"r{g}{c}" for g in range(G // 2) for c in range(3)]
                + [f"x{b}" for b in range(NB)] + [f"r{g}{c}" for g in range(G // 2, G) for c in range(3)])
        AT = {n: i for i, n in enumerate(USES)}
        ONE_COPY = ["al"] + [f"ld{i}" for i in range(KT)]
        HIGHS = {n: i + 1 for i, n in enumerate(USES)}
        LOWS = {n: len([m for m in USES[:i + 1] if m not in ONE_COPY]) for i, n in enumerate(USES)}

        def bank(name):
            return ps[:, AT[name] % 8]

        def place(name):
            u = ps[:, AT[name] % 8]
            if name == "lbt":
                return u[0:RL0, :], lbt_s[:, :, :], LORA0_SCALE
            if name[0] == "c":
                j = 2 * int(name[1])
                return (u[:, 0:2 * NC].rearrange("p (k n) -> p k n", k=2), pc[:, :, j:j + 2, D:QW], 1.0)
            if name.startswith("p3"):
                return u, pc[:, :, int(name[3]), 0:D], 1.0
            if name.startswith("qc"):
                h = "ab".index(name[3])
                return u[:, 0:QP], qc[:, :, int(name[2]), h * QP:(h + 1) * QP], 1.0
            if name[0] == "x":
                return u.rearrange("p (k t) -> p k t", k=KT), xt[:, :, int(name[1])], 1.0
            if name == "b1t":
                return (u.rearrange("p (k q n) -> p k q n", k=KT, q=NB // BG), groups[:, :, :, :, BG * RB:GW], 1.0)
            if name == "b3t":
                return u, b3t[:, :, :], L3_SCALE
            if name[0] == "t":
                t = t1 if name[1] == "1" else t2
                h = "ab".index(name[2])
                return u[:, 0:QP], t[:, :, h * QP:(h + 1) * QP], 1.0
            if name[0] == "r":
                c = int(name[2])
                return u[:, 0:RP], pc[:, :, int(name[1]), c * RP:(c + 1) * RP], 1.0
            raise KeyError(name)

        after = [(len(USES) + i) % 8 for i in range(8)]
        MAIN, SMALL, VT_BANK, HGT_BANK = after[0:2] + after[5:6], after[2:4], after[6], after[7]
        BESIDE = [[["qc0a"], ["qc0b"], ["qc1a"], ["qc1b"], ["qc2a"], ["qc2b"], ["qc3a", "al"]],
                  [["qc3b"], ["b3t"], ["b1t"], ["t1a"], ["t1b"], ["r00"], ["r01"]]]
        groups = qc[:, :, :, QW:RW].rearrange("p s k (q n) -> p s k q n", n=GW)
        l2_cols = groups[:, :, :, :, 0:BG * RB]

        def v_columns(b):
            j = b % BG
            return SEG, SEG + BG * RB - j * (RB - RA)

        block = ctx.enter_context(nc.Block())

        @block.sync
        def _(sp):
            def rows(w):
                return w.rearrange("(k p) n -> p k n", p=P)

            sp.dma_start(cb[:], codebook.partition_broadcast(P)).then_inc(ld_cb, 16)
            sp.dma_start(lb[:], rows(LB0)).then_inc(ld_lb, 16)
            sp.dma_start(la[:], LA0).then_inc(ld_la, 16)
            for i in range(2):
                sp.dma_start(w3[:, 2 * i:2 * i + 2], rows(W3)[:, 2 * i:2 * i + 2]).then_inc(ld_w3[i], 16)
            sp.dma_start(wr[:], Wr).then_inc(ld_wr, 16)
            sp.dma_start(a3[:], A3.rearrange("e r d -> (e r) d")).then_inc(ld_a3, 16)
            sp.dma_start(ids_a[:], adapter_id.rearrange("(a n) -> a n", a=1)).then_inc(ld_ids, 16)
            sp.dma_start(ids_l[:], labeler_id.rearrange("(a n) -> a n", a=1)).then_inc(ld_ids, 16)
            sp.dma_start(r2[:], rows(R2)).then_inc(ld_r2, 16)
            for i in range(2):
                sp.dma_start(w2[:, 2 * i:2 * i + 2], rows(W2)[:, 2 * i:2 * i + 2]).then_inc(ld_w2[i], 16)
            sp.dma_start(slog[:], scale_log.rearrange("(k p) g a -> p k (g a)", p=P)).then_inc(ld_scale, 16)
            for i in range(2):
                sp.dma_start(w0[:, 2 * i:2 * i + 2], rows(W0)[:, 2 * i:2 * i + 2]).then_inc(ld_w0[i], 16)
            sp.wait_ge(ld_ids, 32)
            labeler = [sp.value_load(ids_l[0:1, b:b + 1], min_val=0, max_val=L2.shape[0] - 1) for b in range(NB)]
            for b in range(NB):
                sp.dma_start(l2[:, :, b, :], L2[bass.ds(labeler[b], 1)].rearrange("e (k p) r -> p (e k) r", p=P))\
                  .then_inc(ld_l2, 16)
            adapter = [sp.value_load(ids_a[0:1, b:b + 1], min_val=0, max_val=A1.shape[0] - 1) for b in range(NB)]
            for b in range(NB):
                sp.dma_start(a1[:, :, b, :], A1[bass.ds(adapter[b], 1)].rearrange("e (k p) r -> p (e k) r", p=P))\
                  .then_inc(ld_a1, 16)
            for b in range(NB):
                sp.dma_start(b1[b * RA:(b + 1) * RA, :], B1[bass.ds(adapter[b], 1)].rearrange("e r d -> (e r) d"))\
                  .then_inc(ld_b1, 16)
            for k in range(KT):
                sp.dma_start(b3[:, k], B3.rearrange("e (k p) r -> k p e r", p=P)[k]).then_inc(ld_b3, 16)
            sp.dma_start(x_a[:], x[0:NB // 2].rearrange("b t d -> t b d")).then_inc(ld_x[0], 16)
            sp.wait_ge(filled, AT[f"p3_{KT - 1}"] + 1)
            sp.dma_start(x_b[:], x[NB // 2:NB].rearrange("b t d -> t b d")).then_inc(ld_x[1], 16)
            sp.dma_start(lang_i[:], language_id.partition_broadcast(P)).then_inc(ld_lang, 16)

            sp.wait_ge(low, LOWS["t2b"])
            sp.wait_ge(s_zeroed, 1)
            for s in range(NS):
                for dst, half in ((s_hi[0:RB, s], HI), (s_hi[LO_ROW:LO_ROW + RB, s], HI), (s_lo[0:RB, s], LO)):
                    sp.dma_start(dst.bitcast(F32), t2[0:RB, half].bitcast(F32)).then_inc(s_loaded[s], 16)
            sp.wait_ge(low, LOWS["t1b"])
            for b in range(NB + NOUT):
                if b < NB:
                    if b >= NS:
                        sp.wait_ge(z_main, b - NS + 1)
                    s = b % NS
                    for dst, half in ((s_hi[RB:V, s], HI), (s_hi[LO_ROW + RB:VW, s], HI), (s_lo[RB:V, s], LO)):
                        sp.dma_start(dst.bitcast(F32), t1[b * RA:(b + 1) * RA, half].bitcast(F32)).then_inc(s_loaded[s], 16)
                o = b - NOUT
                if o >= 0:
                    sp.wait_ge(out_copied, o + 1)
                    sp.dma_start(out[o], outs[:, o % NOUT]).then_inc(stored[o % NOUT], 16)
            for s in range(NOUT):
                sp.wait_ge(stored[s], 16 * len(range(s, NB, NOUT)))

        @block.gpsimd
        def _(pool):
            pool.memset(ident[:], 0.0).then_inc(made, 1)
            pool.wait_ge(made, 1)
            pool.affine_select(out=ident[:], in_=ident[:], compare_op=ALU.not_equal, fill=1.0, base=0,
                               pattern=[[-1, P]], channel_multiplier=1).then_inc(made, 1)
            pool.wait_ge(made, 2)
            for k in range(KT):
                if k % 2 == 0:
                    pool.wait_ge(ld_w3[k // 2], 16)
                pool.tensor_tensor(w3[:, k, k * P:(k + 1) * P], w3[:, k, k * P:(k + 1) * P], ident[:], ALU.add)\
                    .then_inc(eye3, 1)
            pool.iota(iota_i[:], [[1, E]], base=0, channel_multiplier=0).then_inc(diag_made, 1)
            pool.memset(diag[:], 1.0).then_inc(diag_made, 1)
            pool.wait_ge(diag_made, 2)
            pool.affine_select(out=diag[:], in_=diag[:], compare_op=ALU.is_ge, fill=0.0, base=RB - 1,
                               pattern=[[-P, 2], [RB, NB], [0, RA]], channel_multiplier=-1).then_inc(diag_made, 1)
            pool.wait_ge(diag_made, 3)
            pool.affine_select(out=diag[:], in_=diag[:], compare_op=ALU.is_ge, fill=0.0, base=0,
                               pattern=[[P, 2], [-RB, NB], [0, RA]], channel_multiplier=1).then_inc(diag_made, 1)
            for k in range(KT):
                if k % 2 == 0:
                    pool.wait_ge(ld_w2[k // 2], 16)
                pool.tensor_tensor(w2[:, k, k * P:(k + 1) * P], w2[:, k, k * P:(k + 1) * P], ident[:], ALU.add)\
                    .then_inc(eye2, 1)
            for k in range(KT - 1):
                pool.wait_ge(w2_hi, k + 1)
                pool.tensor_tensor(pc[:, LO, k, QW:XW], w2[:, k], pc[:, HI, k, QW:XW].bitcast(F32), ALU.subtract)\
                    .then_inc(w2_low, 1)
            pool.wait_ge(rs_ready, 1)
            pool.wait_ge(shifted, KT)
            for g in range(1, G):
                pool.tensor_tensor(nrm[:, g], w0[:, :, g * P:(g + 1) * P],
                                   rscale[:, :, g:g + 1].to_broadcast([P, KT, P]), ALU.mult).then_inc(q_n, 1)

            def finish(g):
                cols = w0[:, :, g * P:(g + 1) * P]
                pool.wait_ge(q_err, g + 1)
                pool.tensor_tensor(cols, cols, nrm[:, g], ALU.add).then_inc(q_fin, 1)
                pool.wait_ge(q_fin, 3 * g + 1)
                pool.tensor_tensor(cols, cols, scale[:, :, g:g + 1].to_broadcast([P, KT, P]), ALU.mult)\
                    .then_inc(q_fin, 1)
                pool.wait_ge(q_fin, 3 * g + 2)
                if g == 0:
                    pool.wait_ge(eye_ld, KT)
                pool.tensor_tensor(cols, cols, ld[:, :, g * P:(g + 1) * P], ALU.add).then_inc(q_fin, 1)

            def w0_low(g):
                pool.wait_ge(w0_hi, g + 1)
                cols = slice(g * P, (g + 1) * P)
                pool.tensor_tensor(w0_s[:, LO, :, cols], w0[:, :, cols], w0_s[:, HI, :, cols].bitcast(F32),
                                   ALU.subtract).then_inc(w0_lo, 1)

            for k in range(KT):
                pool.wait_ge(shifted, k + 1)
                pool.tensor_tensor(ld[:, k, k * P:(k + 1) * P], ld[:, k, k * P:(k + 1) * P], ident[:], ALU.add)\
                    .then_inc(eye_ld, 1)

            pool.wait_ge(l2_hi, 2)
            for q in range(NB // BG):
                pool.tensor_tensor(l2_cols[:, LO, :, q], l2[:, :, BG * q:BG * (q + 1)].rearrange("p k b r -> p k (b r)"),
                                   l2_cols[:, HI, :, q].bitcast(F32), ALU.subtract).then_inc(l2_lo, 1)
            pool.wait_ge(a1_hi, 1)
            pool.tensor_tensor(a1_s[:, LO].rearrange("p k n -> p (k n)"),
                               a1[:].rearrange("p k b r -> p (k b r)"),
                               a1_s[:, HI].rearrange("p k n -> p (k n)").bitcast(F32), ALU.subtract)\
                .then_inc(a1_lo, 1)
            own = diag[:].rearrange("p h b r -> p (h b r)")
            al_hi, al_lo = (al_s[:, half].rearrange("p h n -> p (h n)") for half in (HI, LO))
            raw, kept = (al_raw[:, i].rearrange("p h n -> p (h n)") for i in range(2))
            pool.wait_ge(high, HIGHS["al"])
            pool.wait_ge(diag_made, 4)
            pool.tensor_tensor(al_hi, raw, own, ALU.mult).then_inc(al_masked, 1)
            pool.tensor_tensor(kept, raw, own, ALU.mult).then_inc(al_masked, 1)
            pool.wait_ge(al_masked, 2)
            pool.tensor_tensor(al_lo, kept, al_hi.bitcast(F32), ALU.subtract).then_inc(al_split, 1)
            finish(0)
            w0_low(0)
            finish(1)
            w0_low(1)
            finish(2)
            w0_low(2)
            pool.wait_ge(filled, AT["al"] + 1)
            pool.wait_ge(w0_lo, 3)
            pool.memset(s_hi[RB:LO_ROW].bitcast(F32), 0.0).then_inc(s_zeroed, 1)
            pool.wait_ge(s_zeroed, 1)
            finish(3)
            w0_low(3)

        @block.scalar
        def _(act):
            def hi_of(name):
                act.wait_ge(filled, AT[name] + 1)
                if name == "al":
                    act.activation(al_raw[:, 0].rearrange("p h n -> p (h n)"), bank(name)[:, 0:2 * P], ACT.Copy)\
                        .then_inc(high, 1)
                elif name in ONE_COPY:
                    act.activation(ld[:, int(name[2])], bank(name), ACT.Copy).then_inc(high, 1)
                else:
                    src, dst, by = place(name)
                    act.activation(dst[:, HI], src, ACT.Copy, scale=by).then_inc(high, 1)

            def add_step(pair, s):
                for par in range(2):
                    act.wait_ge(q_sum, 14 * pair + 2 * s + par + 1)
                    act.activation(bia[:, par], acc[:, par], ACT.Identity, bias=step[:, 5 - s:6 - s])\
                        .then_inc(q_bias, 1)

            def w0_high(g):
                act.wait_ge(q_fin, 3 * g + 3)
                act.activation(w0_s[:, HI, :, g * P:(g + 1) * P], w0[:, :, g * P:(g + 1) * P], ACT.Copy)\
                    .then_inc(w0_hi, 1)

            act.wait_ge(ld_la, 16)
            act.activation(la_s[:, HI], la[:], ACT.Copy).then_inc(la_hi, 1)
            def w2_high(k):
                act.wait_ge(eye2, k + 1)
                act.activation(pc[:, HI, k, QW:XW], w2[:, k], ACT.Copy).then_inc(w2_hi, 1)

            for n in USES[:AT["c0"]]:
                hi_of(n)
            act.wait_ge(ld_r2, 16)
            act.activation(r2_x[:], r2[:, :, None, :].to_broadcast([P, KT, KT, RB]), ACT.Copy, scale=L2_SCALE)\
                .then_inc(r2_hi, 1)
            w2_high(0)
            act.wait_ge(r2_hi, 1)
            act.activation(r2_s[:, HI], r2_x[:].rearrange("p k c r -> p k (c r)"), ACT.Copy).then_inc(r2_hi, 1)
            w2_high(1)
            hi_of("c0")
            hi_of("c1")
            w2_high(2)
            w2_high(3)
            act.wait_ge(ld_scale, 16)
            act.activation(scale[:], slog[:], ACT.Exp).then_inc(exped, 1)
            for n in ["t2a", "t2b"]:
                hi_of(n)
            act.wait_ge(ld_l2, 16 * NB)
            for q in range(NB // BG):
                act.activation(l2_cols[:, HI, :, q], l2[:, :, BG * q:BG * (q + 1)].rearrange("p k b r -> p k (b r)"),
                               ACT.Copy).then_inc(l2_hi, 1)
            for pair in range(2):
                for s in range(7):
                    if s < 6:
                        add_step(pair, s)
                    if (pair, s) == (0, 3):
                        act.wait_ge(ld_a1, 16 * NB)
                        act.activation(a1_s[:, HI], a1[:].rearrange("p k b r -> p k (b r)"), ACT.Copy)\
                            .then_inc(a1_hi, 1)
                    if pair == 1 and s in (3, 6):
                        w0_high(s // 6)
                    for n in BESIDE[pair][s]:
                        hi_of(n)
            for n in USES[AT["r02"]:]:
                hi_of(n)
                if n == "r10":
                    w0_high(2)
                if n == "x7":
                    w0_high(3)

            def v_high(b):
                act.wait_ge(small_done, b + 1)
                if b >= 2:
                    act.wait_ge(vt_up, b - 1)
                l_at, a_at = v_columns(b)
                small = ps[:, SMALL[b % 2]]
                act.activation(vn[:, b % 2, 0:RB], small[:, l_at:l_at + RB], ACT.Copy).then_inc(v_hi, 1)
                act.activation(vn[:, b % 2, RB:V], small[:, a_at:a_at + RA], ACT.Copy).then_inc(v_hi, 1)

            def v_turned(b):
                act.wait_ge(vt_up, b + 1)
                if b >= 2:
                    act.wait_ge(z_main, b - 1)
                act.activation(vt[0:VW, b % 2], ps[0:VW, VT_BANK, 0:T], ACT.Copy).then_inc(vt_copied, 1)

            def gate_exp(b):
                act.wait_ge(gap_ready, b + 1)
                act.activation(gw[:, 1:2], gw[:, 0:1], ACT.Exp).then_inc(exp_done, 1)

            def hgt_high(b):
                act.wait_ge(hgt_up, b + 1)
                if b >= 1:
                    act.wait_ge(main_done, b)
                act.activation(hgt[:, HI], ps[:, HGT_BANK, 0:T], ACT.Copy).then_inc(hgt_hi, 1)

            def out_copy(b):
                act.wait_ge(main_done, b + 1)
                if b >= NOUT:
                    act.wait_ge(stored[b % NOUT], 16 * (b // NOUT))
                act.activation(outs[:, b % NOUT], ps[:, MAIN[b % 3]], ACT.Copy).then_inc(out_copied, 1)

            v_high(0)
            v_turned(0)
            v_high(1)
            gate_exp(0)
            v_turned(1)
            hgt_high(0)
            for b in range(1, NB):
                gate_exp(b)
                out_copy(b - 1)
                if b + 1 < NB:
                    v_high(b + 1)
                    v_turned(b + 1)
                hgt_high(b)
            out_copy(NB - 1)

        @block.vector
        def _(dve):
            chain = [0]

            def link(ins):
                chain[0] += 1
                ins.then_inc(dve_chain, 1)
                dve.wait_ge(dve_chain, chain[0])

            def lo_of(name):
                if name in ONE_COPY:
                    return
                dve.wait_ge(high, HIGHS[name])
                src, dst, by = place(name)
                hi = dst[:, HI].bitcast(F32)
                if by == 1.0:
                    dve.tensor_tensor(dst[:, LO], src, hi, ALU.subtract).then_inc(low, 1)
                else:
                    dve.scalar_tensor_tensor(dst[:, LO], src, by, hi, ALU.mult, ALU.subtract).then_inc(low, 1)

            dve.wait_ge(ld_cb, 16)
            link(dve.tensor_reduce(tiny[:, 0:1], cb[:], AX.X, ALU.max))
            link(dve.tensor_reduce(tiny[:, 1:2], cb[:], AX.X, ALU.min))
            link(dve.tensor_scalar(tiny[:, 1:2], tiny[:, 1:2], -1.0, 1e-8, ALU.mult, ALU.max))
            link(dve.tensor_tensor(tiny[:, 0:1], tiny[:, 0:1], tiny[:, 1:2], ALU.max))
            link(dve.reciprocal(tiny[:, 2:3], tiny[:, 0:1]))
            link(dve.tensor_scalar(cbn[:], cb[:], tiny[:, 2:3], None, ALU.mult))
            link(dve.tensor_tensor(thr[:, 0:7], cbn[:, 0:7], cbn[:, 1:8], ALU.add))
            link(dve.tensor_scalar(thr[:, 0:7], thr[:, 0:7], 0.5, None, ALU.mult))
            link(dve.tensor_tensor(step[:, 0:7], cbn[:, 1:8], cbn[:, 0:7], ALU.subtract))
            dve.wait_ge(la_hi, 1)
            dve.tensor_tensor(la_s[:, LO], la[:], la_s[:, HI].bitcast(F32), ALU.subtract).then_inc(la_lo, 1)
            lo_of("lbt")
            link(dve.tensor_tensor(thr[:, 2:3], thr[:, 2:3], thr[:, 1:2], ALU.max))
            link(dve.tensor_tensor(thr[:, 2:3], thr[:, 2:3], thr[:, 3:4], ALU.min))
            link(dve.tensor_tensor(thr[:, 1:2], thr[:, 1:2], thr[:, 3:4], ALU.min))
            link(dve.tensor_tensor(thr[:, 0:1], thr[:, 0:1], thr[:, 1:2], ALU.min))
            link(dve.tensor_tensor(thr[:, 4:5], thr[:, 4:5], thr[:, 5:6], ALU.min))
            link(dve.tensor_tensor(thr[:, 4:5], thr[:, 4:5], thr[:, 3:4], ALU.max))
            link(dve.tensor_tensor(thr[:, 5:6], thr[:, 5:6], thr[:, 3:4], ALU.max))
            link(dve.tensor_tensor(thr[:, 6:7], thr[:, 6:7], thr[:, 5:6], ALU.max))
            for n in USES[AT["p3_0"]:AT["c0"]]:
                lo_of(n)
            dve.wait_ge(r2_hi, 2)
            dve.tensor_tensor(r2_s[:, LO], r2_x[:].rearrange("p k c r -> p k (c r)"), r2_s[:, HI].bitcast(F32),
                              ALU.subtract).then_inc(r2_lo, 1)
            lo_of("c0")
            lo_of("c1")
            dve.wait_ge(w2_hi, KT)
            dve.tensor_tensor(pc[:, LO, KT - 1, QW:XW], w2[:, KT - 1], pc[:, HI, KT - 1, QW:XW].bitcast(F32),
                              ALU.subtract).then_inc(w2_last_lo, 1)
            dve.wait_ge(exped, 1)
            dve.reciprocal(rscale[:], scale[:]).then_inc(rs_ready, 1)
            dve.wait_ge(rs_ready, 1)
            for k in range(KT):
                if k % 2 == 0:
                    dve.wait_ge(ld_w0[k // 2], 16)
                if k == 0:
                    dve.wait_ge(high, HIGHS[f"ld{KT - 1}"])
                dve.tensor_tensor(w0[:, k], w0[:, k], ld[:, k], ALU.add).then_inc(shifted, 1)

            def level(pair, s):
                i = 6 - s
                for par in range(2):
                    n = nrm[:, 2 * pair + par].rearrange("p k n -> p (k n)")
                    a = acc[:, par].rearrange("p k n -> p (k n)")
                    if s == 0:
                        dve.wait_ge(*((q_n, 2 * pair + par) if pair + par else (q_n0, 1)))
                        if pair:
                            dve.wait_ge(q_err, par + 1)
                        dve.tensor_scalar(a, n, thr[:, i:i + 1], step[:, i:i + 1], ALU.is_gt, ALU.mult)\
                            .then_inc(q_sum, 1)
                    else:
                        dve.wait_ge(q_bias, 12 * pair + 2 * (s - 1) + par + 1)
                        b = bia[:, par].rearrange("p k n -> p (k n)")
                        dve.scalar_tensor_tensor(a, n, thr[:, i:i + 1], b, ALU.is_gt, ALU.mult).then_inc(q_sum, 1)

            def error_of(pair):
                for par in range(2):
                    g = 2 * pair + par
                    dve.wait_ge(q_sum, 14 * pair + 12 + par + 1)
                    dve.scalar_tensor_tensor(w0[:, :, g * P:(g + 1) * P], acc[:, par], cbn[:, 0:1], nrm[:, g],
                                             ALU.add, ALU.subtract).then_inc(q_err, 1)

            late = ["t2a", "t2b"]
            for pair in range(2):
                if pair == 0:
                    dve.wait_ge(shifted, KT)
                    dve.tensor_tensor(nrm[:, 0], w0[:, :, 0:P], rscale[:, :, 0:1].to_broadcast([P, KT, P]), ALU.mult)\
                        .then_inc(q_n0, 1)
                for s in range(7):
                    level(pair, s)
                    for n in late:
                        lo_of(n)
                    late = BESIDE[pair][s]
                error_of(pair)
            for n in late:
                lo_of(n)
            dve.wait_ge(q_err, G)
            link(dve.memset(vn[:].bitcast(F32), 0.0))
            dve.wait_ge(ld_lang, 16)
            dve.wait_ge(diag_made, 1)
            link(dve.tensor_copy(lang[:], lang_i[:]))
            link(dve.tensor_copy(iota[:], iota_i[:]))
            for b in range(NB):
                link(dve.tensor_scalar(lbias[:, b], iota[:], lang[:, b:b + 1], LANG_BIAS, ALU.is_equal, ALU.mult))
            for n in USES[AT["r02"]:]:
                lo_of(n)

            def v_low(b):
                l_at, a_at = v_columns(b)
                small = ps[:, SMALL[b % 2]]
                dve.wait_ge(v_hi, 2 * b + 2)
                dve.tensor_tensor(vn[:, b % 2, LO_ROW:LO_ROW + RB], small[:, l_at:l_at + RB],
                                  vn[:, b % 2, 0:RB].bitcast(F32), ALU.subtract).then_inc(v_lo, 1)
                dve.tensor_tensor(vn[:, b % 2, LO_ROW + RB:VW], small[:, a_at:a_at + RA],
                                  vn[:, b % 2, RB:V].bitcast(F32), ALU.subtract).then_inc(v_lo, 1)

            def hgt_low(b):
                dve.wait_ge(hgt_hi, b + 1)
                dve.tensor_tensor(hgt[:, LO], ps[:, HGT_BANK, 0:T], hgt[:, HI].bitcast(F32), ALU.subtract)\
                    .then_inc(hgt_lo, 1)

            def gates(b):
                small = ps[:, SMALL[b % 2], SEG - NC:SEG]
                dve.wait_ge(z_small, b + 1)
                link(dve.tensor_tensor(lg[:], small[:, 0:E], lbias[:, b], ALU.add))
                link(dve.max(top[:], lg[:]))
                dve.tensor_tensor(gw[:, 0:1], top[:, 1:2], top[:, 0:1], ALU.subtract).then_inc(gap_ready, 1)
                link(dve.max_index(top_i[:], top[:], lg[:]))
                link(dve.tensor_copy(top_f[:], top_i[:]))
                dve.wait_ge(exp_done, b + 1)
                link(dve.tensor_scalar(gw[:, 2:3], gw[:, 1:2], 1.0, None, ALU.add))
                link(dve.reciprocal(gw[:, 3:4], gw[:, 2:3]))
                link(dve.tensor_tensor(gw[:, 4:5], gw[:, 1:2], gw[:, 3:4], ALU.mult))
                link(dve.tensor_scalar(gate[:, 0], iota[:], top_f[:, 0:1], gw[:, 3:4], ALU.is_equal, ALU.mult))
                link(dve.tensor_scalar(gate[:, 1], iota[:], top_f[:, 1:2], gw[:, 4:5], ALU.is_equal, ALU.mult))
                link(dve.tensor_tensor(gate[:, 2], gate[:, 0], gate[:, 1], ALU.add))
                if b >= 2:
                    dve.wait_ge(hgt_up, b - 1)
                dve.tensor_tensor(hg[:, b % 2].rearrange("p (e r) -> p e r", e=E),
                                  small[:, E:NC].rearrange("p (e r) -> p e r", e=E),
                                  gate[:, 2, :, None].to_broadcast([P, E, RE]), ALU.mult).then_inc(hg_ready, 1)

            v_low(0)
            v_low(1)
            for b in range(NB):
                gates(b)
                if 1 <= b < NB - 1:
                    v_low(b + 1)
                hgt_low(b)

        @block.tensor
        def _(pe):
            def use(name):
                if AT[name] >= 8:
                    before = USES[AT[name] - 8]
                    if before in ONE_COPY:
                        pe.wait_ge(high, HIGHS[before])
                    else:
                        pe.wait_ge(low, LOWS[before])

            def split(name):
                pe.wait_ge(low, LOWS[name])

            def product(dst, terms, last=True):
                n = 0
                for lhs, rhs in terms:
                    for a, b in PASSES:
                        mm = pe.matmul(dst, lhs(a), rhs(b), start=(n == 0), stop=(n == 3 * len(terms) - 1))
                        n += 1
                return mm

            pe.wait_ge(made, 2)
            for k in range(WARM_UPS):
                pe.transpose(bank("p3_2")[:, 0:P], ident[:], ident[:])
            use("lbt")
            pe.wait_ge(ld_lb, 16)
            for k in range(KT):
                mm = pe.transpose(bank("lbt")[0:RL0, k * P:(k + 1) * P], lb[:, k], ident[:])
            mm.then_inc(filled, 1)
            def ld_block(k):
                use(f"ld{k}")
                product(bank(f"ld{k}"), [(lambda s: lbt_s[:, s, k * P:(k + 1) * P], lambda s: la_s[:, s])])\
                    .then_inc(filled, 1)

            for k in range(WARM_AGAIN):
                pe.transpose(bank("p3_2")[:, 0:P], ident[:], ident[:])
            split("lbt")
            pe.wait_ge(la_lo, 1)
            for k in range(KT):
                ld_block(k)
            for m in range(KT):
                use(f"p3_{m}")
                pe.wait_ge(eye3, KT)
                for k in range(KT):
                    mm = pe.transpose(bank(f"p3_{m}")[:, k * P:(k + 1) * P], w3[:, k, m * P:(m + 1) * P], ident[:])
                mm.then_inc(filled, 1)
            pe.wait_ge(ld_wr, 16)
            pe.wait_ge(ld_a3, 16)
            for j in range(2):
                use(f"c{j}")
                for i in range(2):
                    k = 2 * j + i
                    pe.transpose(bank(f"c{j}")[:, i * NC:i * NC + E], wr[:, k * P:(k + 1) * P], ident[0:E, 0:E])
                    mm = pe.transpose(bank(f"c{j}")[:, i * NC + E:(i + 1) * NC], a3[:, k * P:(k + 1) * P], ident[:])
                mm.then_inc(filled, 1)

            def w2_cols(m, i):
                return lambda s: pc[:, s, m, QW + i * P:QW + (i + 1) * P]

            def p3c(m, h):
                return lambda s: pc[:, s, m, h * QP:(h + 1) * QP]

            def qcv(m, a, b):
                return lambda s: qc[:, s, m, a:b]

            pe.wait_ge(r2_lo, 1)
            for h in range(2):
                name = "t2" + "ab"[h]
                use(name)
                split(("p3_3", "c1")[h])
                product(bank(name)[:, 0:QP], [(lambda s, m=m: r2_s[:, s, m], p3c(m, h)) for m in range(KT)])\
                    .then_inc(filled, 1)

            def qc_block(i, h):
                name = f"qc{i}" + "ab"[h]
                use(name)
                product(bank(name)[:, 0:QP], [(w2_cols(m, i), p3c(m, h)) for m in range(KT)]).then_inc(filled, 1)

            pe.wait_ge(w2_last_lo, 1)
            pe.wait_ge(w2_low, KT - 1)
            for i in range(KT - 1):
                qc_block(i, 0)
                qc_block(i, 1)
            qc_block(KT - 1, 0)
            use("al")
            pe.wait_ge(l2_lo, NB // BG)
            pe.wait_ge(a1_lo, 1)
            for q in range(NB // BG):
                mm = product(bank("al")[:, q * P:(q + 1) * P],
                             [(lambda s, k=k, q=q: l2_cols[:, s, k, q], lambda s, k=k: a1_s[:, s, k])
                              for k in range(KT)])
            mm.then_inc(filled, 1)
            qc_block(KT - 1, 1)
            use("b3t")
            pe.wait_ge(ld_b3, 16 * KT)
            for k in range(KT):
                mm = pe.transpose(bank("b3t")[:, k * P:(k + 1) * P], b3[:, k].rearrange("p e r -> p (e r)"), ident[:])
            mm.then_inc(filled, 1)
            use("b1t")
            pe.wait_ge(ld_b1, 16 * NB)
            for k in range(KT):
                mm = pe.transpose(bank("b1t")[:, k * P:(k + 1) * P], b1[:, k * P:(k + 1) * P], ident[:])
            mm.then_inc(filled, 1)
            split("qc3b")
            for h in range(2):
                name = "t1" + "ab"[h]
                a, b = h * QP, (h + 1) * QP
                use(name)
                if h == 0:
                    pe.wait_ge(al_split, 1)
                product(bank(name)[:, 0:QP],
                        [(lambda s, m=m: a1_s[:, s, m], qcv(m, a, b)) for m in range(KT)]
                        + [(lambda s, q=q: al_s[:, s, q], lambda s, a=a, b=b: t2[:, s, a:b]) for q in range(2)])\
                    .then_inc(filled, 1)

            def r_block(g):
                pe.wait_ge(w0_lo, g + 1)
                for c in range(3):
                    use(f"r{g}{c}")
                    product(bank(f"r{g}{c}")[:, 0:RP],
                            [(lambda s, m=m: w0_s[:, s, m, g * P:(g + 1) * P], qcv(m, c * RP, (c + 1) * RP))
                             for m in range(KT)]).then_inc(filled, 1)

            split("b1t")
            r_block(0)
            r_block(1)
            for b in range(NB):
                use(f"x{b}")
                if b % 4 == 0:
                    pe.wait_ge(ld_x[b // 4], 16)
                src = (x_a, x_b)[b // 4]
                for k in range(KT):
                    mm = pe.transpose(bank(f"x{b}")[:, k * P:(k + 1) * P], src[:, b % 4, k * P:(k + 1) * P], ident[:])
                mm.then_inc(filled, 1)
            r_block(2)
            r_block(3)

            row = 2 * KT * XW

            def small_cols(b, k, s):
                base = pc[:, s, k, QW - SEG:QW]
                there = SEG + b // BG * GW + b % BG * RB
                return bass.AP(base.tensor, base.offset, [[row, P], [there, 2], [1, SEG]])

            def small(b, ks):
                if b >= 2 and 0 in ks:
                    pe.wait_ge(hg_ready, b - 1)
                for k in ks:
                    for n, (u, w) in enumerate(PASSES):
                        mm = pe.matmul(ps[:, SMALL[b % 2], 0:2 * SEG], xt[:, u, b, k], small_cols(b, k, w),
                                       start=(k == 0 and n == 0), stop=(k == KT - 1 and n == 2))
                if KT - 1 in ks:
                    mm.then_inc(small_done, 1)

            def main(b, ks):
                if b >= 3 and 0 in ks:
                    pe.wait_ge(out_copied, b - 2)
                for k in ks:
                    for n, (u, w) in enumerate(PASSES):
                        pe.matmul(ps[:, MAIN[b % 3]], xt[:, u, b, k], pc[:, w, k, 0:D],
                                  start=(k == 0 and n == 0), stop=False, skip_group_check=True)

            def turn_v(b):
                pe.wait_ge(v_lo, 2 * b + 2)
                if b >= 1:
                    pe.wait_ge(vt_copied, b)
                pe.transpose(ps[0:VW, VT_BANK, 0:T].bitcast(F32), vn[:, b % 2, 0:VW].bitcast(F32), ident[:])\
                    .then_inc(vt_up, 1)

            def add_v(b, dst, a, e):
                s = b % NS
                pe.matmul(dst, vt[0:VW, b % 2], s_hi[:, s, a:e], start=False, stop=False, skip_group_check=True)
                return pe.matmul(dst, vt[0:V, b % 2], s_lo[:, s, a:e], start=False, stop=(a > 0),
                                 skip_group_check=True)

            def add_v_small(b):
                pe.wait_ge(vt_copied, b + 1)
                pe.wait_ge(s_loaded[b % NS], 48 * (b // NS + 2))
                add_v(b, ps[:, SMALL[b % 2], SEG - NC:SEG], D, QW).then_inc(z_small, 1)

            def add_v_main(b):
                add_v(b, ps[:, MAIN[b % 3]], 0, D).then_inc(z_main, 1)

            def turn_hg(b):
                pe.wait_ge(hg_ready, b + 1)
                if b >= 1:
                    pe.wait_ge(hgt_lo, b)
                pe.transpose(ps[:, HGT_BANK, 0:T], hg[:, b % 2], ident[:]).then_inc(hgt_up, 1)

            def add_experts(b):
                pe.wait_ge(hgt_lo, b + 1)
                for n, (u, w) in enumerate(PASSES):
                    mm = pe.matmul(ps[:, MAIN[b % 3]], hgt[:, u], b3t[:, w], start=False, stop=(n == 2),
                                   skip_group_check=True)
                mm.then_inc(main_done, 1)

            split(f"r{G - 2}2")
            small(0, range(KT - 1))
            main(0, range(KT - 1))
            split(f"r{G - 1}2")
            small(0, [KT - 1])
            main(0, [KT - 1])
            turn_v(0)
            small(1, range(KT))
            add_v_small(0)
            add_v_main(0)
            turn_v(1)
            main(1, range(3))
            add_v_small(1)
            turn_hg(0)
            main(1, [3])
            add_v_main(1)
            add_experts(0)
            for b in range(2, NB):
                small(b, range(KT))
                main(b, [0])
                turn_v(b)
                turn_hg(b - 1)
                main(b, [1])
                add_v_small(b)
                add_experts(b - 1)
                main(b, [2, 3])
                add_v_main(b)
            turn_hg(NB - 1)
            add_experts(NB - 1)


_INS = ["x", "condB_codebook", "itok_B_3_7", "itok_B_0_2", "itok_B_0_7", "L0_cond_weight", "L0_cond_scale_log",
        "L0_cond_lora_A", "L0_cond_lora_B", "L1_cond_A", "L1_cond_B", "L2_cond_W", "L2_cond_lora_A",
        "L2_cond_lora_B_w", "L3_cond_W", "L3_cond_Wr", "L3_cond_A", "L3_cond_B"]


def kernel(**inputs):
    import numpy as np
    import concourse.bacc as bacc
    from concourse.bass_utils import run_bass_kernel_spmd

    nc = bacc.Bacc("TRN2", target_bir_lowering=False, num_devices=1)
    arrays, args = {}, []
    for name in _INS:
        a = np.ascontiguousarray(inputs[name])
        arrays[f"in_{name}"] = a
        args.append(nc.dram_tensor(f"in_{name}", a.shape, mybir.dt.from_np(a.dtype), kind="ExternalInput").ap())
    out = nc.dram_tensor("out_dram", inputs["x"].shape, F32, kind="ExternalOutput").ap()
    layer_chain(nc, *args, out)
    r = run_bass_kernel_spmd(nc, [arrays], core_ids=[0])
    return r.results[0]["out_dram"]
```

```python
from contextlib import ExitStack

import concourse.bass as bass
from concourse import mybir

F32 = mybir.dt.float32
F32R = mybir.dt.float32r
I32 = mybir.dt.int32
U32 = mybir.dt.uint32
ALU = mybir.AluOpType
ACT = mybir.ActivationFunctionType
AX = mybir.AxisListType

P = 128
HI, LO = 0, 1
PASSES = ((HI, HI), (HI, LO), (LO, HI))


def layer_chain(nc, x, codebook, adapter_id, labeler_id, language_id, W0, scale_log, LA0, LB0, A1, B1, W2, L2, R2,
                W3, Wr, A3, B3, out):
    NB, T, D = x.shape
    KT = D // P
    G = KT
    RL0 = LA0.shape[0]
    RA = A1.shape[2]
    RB = L2.shape[2]
    E, RE = A3.shape[0], A3.shape[1]
    NC = E + E * RE
    V = RB + RA
    QW = D + NC
    RW = QW + NB * V
    QP = QW // 2
    RP = RW // 3
    BG = P // RB
    GW = BG * V
    SEG = (BG * RB + RA)
    XW = QW + D
    NCB = codebook.shape[0]
    assert (T, D, NC, V, RB * KT, NCB, E) == (P, 512, 136, 48, P, 8, 8) and RW % 3 == 0
    LORA0_SCALE, L2_SCALE, L3_SCALE, LANG_BIAS = 0.5, 0.5, 2.0, 5.0
    LO_ROW = 64
    VW = LO_ROW + V
    NS, NOUT = 3, 3
    WARM_UPS, WARM_AGAIN = 13, 15

    ctx = ExitStack()
    with ctx:
        at = [(nc.sbuf_base + 63) // 64 * 64]

        def put(name, shape, dt, offset):
            return nc.alloc_sbuf_tensor_at(name, shape, dt, offset=offset)

        def sb(name, shape, dt=F32):
            n = 4
            for s in shape[1:]:
                n *= s
            offset = at[0]
            at[0] += (n + 63) // 64 * 64
            assert at[0] <= nc.sbuf_top, (name, at[0], nc.sbuf_top)
            return put(name, shape, dt, offset), offset

        w0, w0_at = sb("w0", [P, KT, D])
        w2, w2_at = sb("w2", [P, KT, D])
        w3, w3_at = sb("w3", [P, KT, D])
        x_a, _ = sb("x_first_half", [P, NB // 2, D])
        x_b = put("x_second_half", [P, NB // 2, D], F32, w3_at)
        early_at = at[0]
        lb, _ = sb("lb", [P, KT, RL0])
        la, _ = sb("la", [RL0, D])
        la_s, _ = sb("la_split", [RL0, 2, D], F32R)
        lbt_s, _ = sb("lbt_split", [RL0, 2, D], F32R)
        a3, _ = sb("a3", [P, D])
        b1, _ = sb("b1", [P, D])
        l2, _ = sb("l2", [P, KT, NB, RB])
        early_end = at[0]
        r2, _ = sb("r2", [P, KT, RB])
        b3, _ = sb("b3", [P, KT, E, RE])
        xt, xt_at = sb("xt_split", [P, 2, NB, KT, T], F32R)
        kb = D * 4
        r2_s = put("r2_split", [P, 2, KT, P], F32R, xt_at + kb)
        a1 = put("a1", [P, KT, NB, RA], F32, xt_at + 3 * kb)
        a1_s = put("a1_split", [P, 2, KT, P], F32R, xt_at + 4 * kb)
        wr = put("wr", [E, D], F32, xt_at + 8 * kb)
        al_kept = put("al_kept", [P, 2, P], F32, xt_at + 6 * kb)
        al_s = put("al_split", [P, 2, 2, P], F32R, xt_at + 7 * kb)
        w0_s, _ = sb("w0_split", [P, 2, KT, D], F32R)
        pc, _ = sb("p3c_w2_then_r", [P, 2, KT, XW], F32R)
        qc, _ = sb("qc_split", [P, 2, KT, RW], F32R)
        b3t, _ = sb("b3t_split", [P, 2, D], F32R)
        t1 = put("t1_split", [P, 2, QW], F32R, w2_at)
        t2, _ = sb("t2_split", [P, 2, QW], F32R)
        s_hi = put("s_hi", [VW, NS, QW], F32R, early_at)
        s_lo = put("s_lo", [V, NS, QW], F32R, early_at + NS * QW * 4)
        assert early_end - early_at >= 2 * NS * QW * 4, (early_end - early_at)
        outs = put("out_rows", [P, NOUT, D], F32, w0_at)
        ld, _ = sb("ld", [P, KT, D])
        nrm, _ = sb("normalized", [P, G, KT, P])
        acc, acc_at = sb("level_sum", [P, 2, KT, P])
        bia, _ = sb("level_biased", [P, 2, KT, P])
        ident, _ = sb("ident", [P, P])
        diag, _ = sb("diag", [P, 2, NB, RA])
        iota_i, _ = sb("iota_i", [P, E], I32)
        iota, _ = sb("iota", [P, E])
        ids_a, _ = sb("ids_adapter", [1, NB], I32)
        ids_l, _ = sb("ids_labeler", [1, NB], I32)
        lang_i, _ = sb("lang_i", [P, NB], I32)
        lang, _ = sb("lang", [P, NB])
        lbias, _ = sb("lang_bias", [P, NB, E])
        cb, _ = sb("cb", [P, NCB])
        cbn, _ = sb("cbn", [P, NCB])
        thr, _ = sb("thr", [P, NCB])
        step, _ = sb("step", [P, NCB])
        tiny, _ = sb("tiny", [P, 4])
        slog, _ = sb("slog", [P, KT, G])
        scale, _ = sb("scale", [P, KT, G])
        rscale, _ = sb("rscale", [P, KT, G])
        vn = put("v_rows", [P, 2, P], F32R, acc_at)
        vt = put("v_cols", [P, 2, T], F32R, acc_at + 2 * P * 4)
        lg, _ = sb("logits", [P, E])
        top, _ = sb("top", [P, 8])
        top_i, _ = sb("top_i", [P, 8], U32)
        top_f, _ = sb("top_f", [P, 8])
        gw, _ = sb("gate_weights", [P, 8])
        gate, _ = sb("gate", [P, 3, E])
        hg = put("h_gated", [P, 2, E * RE], F32, acc_at + 4 * P * 4)
        hgt = put("hgt_split", [P, 2, T], F32R, acc_at + 6 * P * 4)

        ps = ctx.enter_context(nc.psum_tensor("ps", [P, 8, 512], F32))

        def sem(name):
            return ctx.enter_context(nc.semaphore(name))

        ld_ids, ld_lang, ld_cb, ld_scale, ld_lb, ld_la = (
            sem(f"loaded_{n}") for n in ("ids", "lang", "cb", "scale", "lb", "la"))
        ld_w3 = [sem(f"loaded_w3_{i}") for i in range(2)]
        ld_w2 = [sem(f"loaded_w2_{i}") for i in range(2)]
        ld_w0 = [sem(f"loaded_w0_{i}") for i in range(2)]
        ld_wr, ld_a3, ld_b3, ld_r2, ld_b1, ld_l2, ld_a1 = (
            sem(f"loaded_{n}") for n in ("wr", "a3", "b3", "r2", "b1", "l2", "a1"))
        ld_x = [sem(f"loaded_x_{i}") for i in range(2)]
        s_loaded = [sem(f"s_loaded_{i}") for i in range(NS)]
        stored = [sem(f"stored_{i}") for i in range(NOUT)]
        made = sem("constants_made")
        s_zeroed = sem("s_rows_zeroed")
        eye3, eye2 = sem("w3_plus_identity"), sem("w2_plus_identity")
        shifted, eye_ld = sem("w0_plus_ld"), sem("ld_plus_identity")
        diag_made = sem("diag_made")
        w2_hi, w2_low = sem("w2_hi"), sem("w2_lo")
        la_hi, la_lo = sem("la_hi"), sem("la_lo")
        a1_hi, a1_lo = sem("a1_hi"), sem("a1_lo")
        l2_hi, l2_lo = sem("l2_hi"), sem("l2_lo")
        r2_hi, r2_lo = sem("r2_hi"), sem("r2_lo")
        al_masked = sem("al_masked")
        filled, high, low = sem("bank_filled"), sem("bank_high"), sem("bank_low")
        exped, dve_chain = sem("scale_exp"), sem("dve_chain")
        rs_ready, q_n0 = sem("rscale_ready"), sem("quant_first_normal")
        q_n, q_sum, q_bias, q_err, q_fin = (sem(f"quant_{n}") for n in ("normal", "sum", "bias", "err", "fin"))
        w0_hi, w0_lo = sem("w0_hi"), sem("w0_lo")
        small_done, v_hi, v_lo, vt_up, vt_copied, z_small, z_main = (
            sem(n) for n in ("small_done", "v_hi", "v_lo", "v_turned", "v_copied", "z_small", "z_main"))
        gap_ready, exp_done, hg_ready, hgt_up, hgt_hi, hgt_lo, main_done, out_copied = (
            sem(n) for n in ("gap_ready", "exp_done", "hg_ready", "hg_turned", "hgt_hi", "hgt_lo", "main_done",
                             "out_copied"))

        USES = (["lbt"] + [f"p3_{i}" for i in range(KT)] + ["c0", "c1"] + [f"ld{i}" for i in range(KT)] + ["t2a", "t2b"]
                + [f"qc{i}{h}" for i in range(KT) for h in "ab"]
                + ["al", "b1t", "b3t", "t1a", "t1b"] + [f"r{g}{c}" for g in range(G // 2) for c in range(3)]
                + [f"x{b}" for b in range(NB)] + [f"r{g}{c}" for g in range(G // 2, G) for c in range(3)])
        AT = {n: i for i, n in enumerate(USES)}
        NO_LOW = [f"ld{i}" for i in range(KT)]
        HIGHS = {n: len([m for m in USES[:i + 1] if m != "al"]) for i, n in enumerate(USES)}
        LOWS = {n: len([m for m in USES[:i + 1] if m not in NO_LOW]) for i, n in enumerate(USES)}

        def bank(name):
            return ps[:, AT[name] % 8]

        def place(name):
            u = ps[:, AT[name] % 8]
            if name == "lbt":
                return u[0:RL0, :], lbt_s[:, :, :], LORA0_SCALE
            if name[0] == "c":
                j = 2 * int(name[1])
                return (u[:, 0:2 * NC].rearrange("p (k n) -> p k n", k=2), pc[:, :, j:j + 2, D:QW], 1.0)
            if name.startswith("p3"):
                return u, pc[:, :, int(name[3]), 0:D], 1.0
            if name.startswith("qc"):
                h = "ab".index(name[3])
                return u[:, 0:QP], qc[:, :, int(name[2]), h * QP:(h + 1) * QP], 1.0
            if name[0] == "x":
                return u.rearrange("p (k t) -> p k t", k=KT), xt[:, :, int(name[1])], 1.0
            if name == "b1t":
                return (u.rearrange("p (k q n) -> p k q n", k=KT, q=NB // BG), groups[:, :, :, :, BG * RB:GW], 1.0)
            if name == "b3t":
                return u, b3t[:, :, :], L3_SCALE
            if name[0] == "t":
                t = t1 if name[1] == "1" else t2
                h = "ab".index(name[2])
                return u[:, 0:QP], t[:, :, h * QP:(h + 1) * QP], 1.0 if name[1] == "1" else L2_SCALE
            if name[0] == "r":
                c = int(name[2])
                return u[:, 0:RP], pc[:, :, int(name[1]), c * RP:(c + 1) * RP], 1.0
            raise KeyError(name)

        after = [(len(USES) + i) % 8 for i in range(8)]
        MAIN, SMALL, VT_BANK, HGT_BANK = after[0:2] + after[5:6], after[2:4], after[6], after[7]
        BESIDE = [[["qc0a", "qc0b"], ["qc1a"], ["qc1b"], ["qc2a"], ["qc2b"], ["qc3a"], ["qc3b"]],
                  [["al"], ["b1t"], ["b3t"], ["t1a"], ["t1b"], ["r00"], ["r01"]]]
        r2_four = r2[:, :, None, :].to_broadcast([P, KT, KT, RB])
        groups = qc[:, :, :, QW:RW].rearrange("p s k (q n) -> p s k q n", n=GW)
        l2_cols = groups[:, :, :, :, 0:BG * RB]

        def main_parts(b):
            if b < NB - 1:
                return [(MAIN[b % 3], 0, D)]
            return [(MAIN[b % 3], 0, D // 2), (MAIN[(b + 1) % 3], D // 2, D)]

        def v_columns(b):
            j = b % BG
            return SEG, SEG + BG * RB - j * (RB - RA)

        def rows(w):
            return w.rearrange("(k p) n -> p k n", p=P)

        block = ctx.enter_context(nc.Block())

        @block.sync
        def _(sp):
            sp.dma_start(cb[:], codebook.partition_broadcast(P)).then_inc(ld_cb, 16)
            sp.dma_start(lb[:], rows(LB0)).then_inc(ld_lb, 16)
            sp.dma_start(la[:], LA0).then_inc(ld_la, 16)
            for i in range(2):
                sp.dma_start(w3[:, 2 * i:2 * i + 2], rows(W3)[:, 2 * i:2 * i + 2]).then_inc(ld_w3[i], 16)
            sp.dma_start(wr[:], Wr).then_inc(ld_wr, 16)
            sp.dma_start(a3[:], A3.rearrange("e r d -> (e r) d")).then_inc(ld_a3, 16)
            sp.dma_start(ids_a[:], adapter_id.rearrange("(a n) -> a n", a=1)).then_inc(ld_ids, 16)
            sp.dma_start(ids_l[:], labeler_id.rearrange("(a n) -> a n", a=1)).then_inc(ld_ids, 16)
            sp.dma_start(r2[:], rows(R2)).then_inc(ld_r2, 16)
            for i in range(2):
                sp.dma_start(w2[:, 2 * i:2 * i + 2], rows(W2)[:, 2 * i:2 * i + 2]).then_inc(ld_w2[i], 16)
            sp.dma_start(slog[:], scale_log.rearrange("(k p) g a -> p k (g a)", p=P)).then_inc(ld_scale, 16)
            for i in range(2):
                sp.dma_start(w0[:, 2 * i:2 * i + 2], rows(W0)[:, 2 * i:2 * i + 2]).then_inc(ld_w0[i], 16)
            sp.wait_ge(ld_ids, 32)
            labeler = [sp.value_load(ids_l[0:1, b:b + 1], min_val=0, max_val=L2.shape[0] - 1) for b in range(NB)]
            for b in range(NB):
                sp.dma_start(l2[:, :, b, :], L2[bass.ds(labeler[b], 1)].rearrange("e (k p) r -> p (e k) r", p=P))\
                  .then_inc(ld_l2, 16)
            adapter = [sp.value_load(ids_a[0:1, b:b + 1], min_val=0, max_val=A1.shape[0] - 1) for b in range(NB)]
            for b in range(NB):
                sp.dma_start(a1[:, :, b, :], A1[bass.ds(adapter[b], 1)].rearrange("e (k p) r -> p (e k) r", p=P))\
                  .then_inc(ld_a1, 16)
            for b in range(NB):
                sp.dma_start(b1[b * RA:(b + 1) * RA, :], B1[bass.ds(adapter[b], 1)].rearrange("e r d -> (e r) d"))\
                  .then_inc(ld_b1, 16)
            for k in range(KT):
                sp.dma_start(b3[:, k], B3.rearrange("e (k p) r -> k p e r", p=P)[k]).then_inc(ld_b3, 16)
            sp.dma_start(x_a[:], x[0:NB // 2].rearrange("b t d -> t b d")).then_inc(ld_x[0], 16)
            sp.wait_ge(filled, AT[f"p3_{KT - 1}"] + 1)
            sp.dma_start(x_b[:], x[NB // 2:NB].rearrange("b t d -> t b d")).then_inc(ld_x[1], 16)
            sp.dma_start(lang_i[:], language_id.partition_broadcast(P)).then_inc(ld_lang, 16)

            sp.wait_ge(low, LOWS["b1t"])
            for s in range(NS):
                for dst, half in ((s_hi[0:RB, s], HI), (s_hi[LO_ROW:LO_ROW + RB, s], HI), (s_lo[0:RB, s], LO)):
                    sp.dma_start(dst.bitcast(F32), t2[0:RB, half].bitcast(F32)).then_inc(s_loaded[s], 16)
            sp.wait_ge(low, LOWS["t1b"])
            sp.wait_ge(s_zeroed, 1)
            for b in range(NB + NOUT):
                if b < NB:
                    if b >= NS:
                        sp.wait_ge(z_main, b - NS + 1)
                    s = b % NS
                    for dst, half in ((s_hi[RB:V, s], HI), (s_hi[LO_ROW + RB:VW, s], HI), (s_lo[RB:V, s], LO)):
                        sp.dma_start(dst.bitcast(F32), t1[b * RA:(b + 1) * RA, half].bitcast(F32)).then_inc(s_loaded[s], 16)
                o = b - NOUT
                if o >= 0:
                    for i, (_, a, e) in enumerate(main_parts(o)):
                        sp.wait_ge(out_copied, o + 1 + i)
                        sp.dma_start(out[o, :, a:e], outs[:, o % NOUT, a:e]).then_inc(stored[o % NOUT], 16)
            for s in range(NOUT):
                sp.wait_ge(stored[s], 16 * sum(len(main_parts(b)) for b in range(s, NB, NOUT)))

        @block.gpsimd
        def _(pool):
            pool.memset(ident[:], 0.0).then_inc(made, 1)
            pool.wait_ge(made, 1)
            pool.affine_select(out=ident[:], in_=ident[:], compare_op=ALU.not_equal, fill=1.0, base=0,
                               pattern=[[-1, P]], channel_multiplier=1).then_inc(made, 1)
            pool.wait_ge(made, 2)
            for k in range(KT):
                if k % 2 == 0:
                    pool.wait_ge(ld_w3[k // 2], 16)
                pool.tensor_tensor(w3[:, k, k * P:(k + 1) * P], w3[:, k, k * P:(k + 1) * P], ident[:], ALU.add)\
                    .then_inc(eye3, 1)
            pool.iota(iota_i[:], [[1, E]], base=0, channel_multiplier=0).then_inc(diag_made, 1)
            pool.memset(diag[:], 1.0).then_inc(diag_made, 1)
            pool.wait_ge(diag_made, 2)
            pool.affine_select(out=diag[:], in_=diag[:], compare_op=ALU.is_ge, fill=0.0, base=RB - 1,
                               pattern=[[-P, 2], [RB, NB], [0, RA]], channel_multiplier=-1).then_inc(diag_made, 1)
            pool.wait_ge(diag_made, 3)
            pool.affine_select(out=diag[:], in_=diag[:], compare_op=ALU.is_ge, fill=0.0, base=0,
                               pattern=[[P, 2], [-RB, NB], [0, RA]], channel_multiplier=1).then_inc(diag_made, 1)
            for k in range(KT):
                if k % 2 == 0:
                    pool.wait_ge(ld_w2[k // 2], 16)
                pool.tensor_tensor(w2[:, k, k * P:(k + 1) * P], w2[:, k, k * P:(k + 1) * P], ident[:], ALU.add)\
                    .then_inc(eye2, 1)
            for k in range(KT):
                pool.wait_ge(w2_hi, k + 1)
                pool.tensor_tensor(pc[:, LO, k, QW:XW], w2[:, k], pc[:, HI, k, QW:XW].bitcast(F32), ALU.subtract)\
                    .then_inc(w2_low, 1)
            pool.wait_ge(rs_ready, 1)
            pool.wait_ge(shifted, KT)
            for g in range(1, G):
                pool.tensor_tensor(nrm[:, g], w0[:, :, g * P:(g + 1) * P],
                                   rscale[:, :, g:g + 1].to_broadcast([P, KT, P]), ALU.mult).then_inc(q_n, 1)

            def add_back(g):
                cols = w0[:, :, g * P:(g + 1) * P]
                pool.wait_ge(q_err, g + 1)
                pool.tensor_tensor(cols, cols, nrm[:, g], ALU.add).then_inc(q_fin, 1)

            def finish(g):
                cols = w0[:, :, g * P:(g + 1) * P]
                pool.wait_ge(q_fin, 3 * g + 1)
                pool.tensor_tensor(cols, cols, scale[:, :, g:g + 1].to_broadcast([P, KT, P]), ALU.mult)\
                    .then_inc(q_fin, 1)
                pool.wait_ge(q_fin, 3 * g + 2)
                if g == 0:
                    pool.wait_ge(eye_ld, KT)
                pool.tensor_tensor(cols, cols, ld[:, :, g * P:(g + 1) * P], ALU.add).then_inc(q_fin, 1)

            def w0_low(g):
                pool.wait_ge(w0_hi, g + 1)
                cols = slice(g * P, (g + 1) * P)
                pool.tensor_tensor(w0_s[:, LO, :, cols], w0[:, :, cols], w0_s[:, HI, :, cols].bitcast(F32),
                                   ALU.subtract).then_inc(w0_lo, 1)

            for k in range(KT):
                pool.wait_ge(shifted, k + 1)
                pool.tensor_tensor(ld[:, k, k * P:(k + 1) * P], ld[:, k, k * P:(k + 1) * P], ident[:], ALU.add)\
                    .then_inc(eye_ld, 1)

            pool.wait_ge(l2_hi, 2)
            for q in range(NB // BG):
                pool.tensor_tensor(l2_cols[:, LO, :, q], l2[:, :, BG * q:BG * (q + 1)].rearrange("p k b r -> p k (b r)"),
                                   l2_cols[:, HI, :, q].bitcast(F32), ALU.subtract).then_inc(l2_lo, 1)
            pool.wait_ge(a1_hi, 1)
            pool.tensor_tensor(a1_s[:, LO].rearrange("p k n -> p (k n)"),
                               a1[:].rearrange("p k b r -> p (k b r)"),
                               a1_s[:, HI].rearrange("p k n -> p (k n)").bitcast(F32), ALU.subtract)\
                .then_inc(a1_lo, 1)
            for g in (0, 2):
                add_back(g)
                finish(g)
                add_back(g + 1)
                w0_low(g)
                finish(g + 1)
                w0_low(g + 1)
            pool.wait_ge(low, LOWS["b1t"])
            pool.wait_ge(w0_lo, G)
            pool.memset(s_hi[RB:LO_ROW].bitcast(F32), 0.0).then_inc(s_zeroed, 1)

        @block.scalar
        def _(act):
            def hi_of(name):
                if name == "al":
                    return
                act.wait_ge(filled, AT[name] + 1)
                if name in NO_LOW:
                    act.activation(ld[:, int(name[2])], bank(name), ACT.Copy).then_inc(high, 1)
                else:
                    src, dst, by = place(name)
                    act.activation(dst[:, HI], src, ACT.Copy, scale=by).then_inc(high, 1)

            def add_step(pair, s):
                for par in range(2):
                    act.wait_ge(q_sum, 14 * pair + 2 * s + par + 1)
                    act.activation(bia[:, par], acc[:, par], ACT.Identity, bias=step[:, 5 - s:6 - s])\
                        .then_inc(q_bias, 1)

            def w0_high(g):
                act.wait_ge(q_fin, 3 * g + 3)
                act.activation(w0_s[:, HI, :, g * P:(g + 1) * P], w0[:, :, g * P:(g + 1) * P], ACT.Copy)\
                    .then_inc(w0_hi, 1)

            act.wait_ge(ld_la, 16)
            act.activation(la_s[:, HI], la[:], ACT.Copy).then_inc(la_hi, 1)
            for n in USES[:AT["c0"]]:
                hi_of(n)
            act.wait_ge(ld_r2, 16)
            act.activation(r2_s[:, HI].rearrange("p k (c r) -> p k c r", r=RB), r2_four, ACT.Copy)\
                .then_inc(r2_hi, 1)
            hi_of("c0")
            hi_of("c1")
            for k in range(KT):
                act.wait_ge(eye2, k + 1)
                act.activation(pc[:, HI, k, QW:XW], w2[:, k], ACT.Copy).then_inc(w2_hi, 1)
                hi_of(f"ld{k}")
                if k == 1:
                    act.wait_ge(ld_scale, 16)
                    act.activation(scale[:], slog[:], ACT.Exp).then_inc(exped, 1)
            for n in ["t2a", "t2b"]:
                hi_of(n)
            act.wait_ge(ld_l2, 16 * NB)
            for q in range(NB // BG):
                act.activation(l2_cols[:, HI, :, q], l2[:, :, BG * q:BG * (q + 1)].rearrange("p k b r -> p k (b r)"),
                               ACT.Copy).then_inc(l2_hi, 1)
            for pair in range(2):
                for s in range(7):
                    if pair == 1 and s in (2, 4):
                        w0_high(s // 4)
                    if s < 6:
                        add_step(pair, s)
                    if (pair, s) == (0, 3):
                        act.wait_ge(ld_a1, 16 * NB)
                        act.activation(a1_s[:, HI], a1[:].rearrange("p k b r -> p k (b r)"), ACT.Copy)\
                            .then_inc(a1_hi, 1)
                    for n in BESIDE[pair][s]:
                        hi_of(n)
            for n in USES[AT["r02"]:]:
                hi_of(n)
                if n == "r10":
                    w0_high(2)
                if n == "x7":
                    w0_high(3)

            def v_high(b):
                act.wait_ge(small_done, b + 1)
                if b >= 2:
                    act.wait_ge(vt_up, b - 1)
                l_at, a_at = v_columns(b)
                small = ps[:, SMALL[b % 2]]
                act.activation(vn[:, b % 2, 0:RB], small[:, l_at:l_at + RB], ACT.Copy).then_inc(v_hi, 1)
                act.activation(vn[:, b % 2, RB:V], small[:, a_at:a_at + RA], ACT.Copy).then_inc(v_hi, 1)

            def v_turned(b):
                act.wait_ge(vt_up, b + 1)
                if b >= 2:
                    act.wait_ge(z_main, b - 1)
                act.activation(vt[0:VW, b % 2], ps[0:VW, VT_BANK, 0:T], ACT.Copy).then_inc(vt_copied, 1)

            def gate_exp(b):
                act.wait_ge(gap_ready, b + 1)
                act.activation(gw[:, 1:2], gw[:, 0:1], ACT.Exp).then_inc(exp_done, 1)

            def hgt_high(b):
                act.wait_ge(hgt_up, b + 1)
                if b >= 1:
                    act.wait_ge(main_done, b)
                act.activation(hgt[:, HI], ps[:, HGT_BANK, 0:T], ACT.Copy).then_inc(hgt_hi, 1)

            def out_copy(b):
                if b >= NOUT:
                    act.wait_ge(stored[b % NOUT], 16 * (b // NOUT))
                for i, (bk, a, e) in enumerate(main_parts(b)):
                    act.wait_ge(main_done, b + 1 + i)
                    act.activation(outs[:, b % NOUT, a:e], ps[:, bk, 0:e - a], ACT.Copy).then_inc(out_copied, 1)

            v_high(0)
            v_high(1)
            v_turned(0)
            v_turned(1)
            gate_exp(0)
            hgt_high(0)
            for b in range(1, NB):
                gate_exp(b)
                if b == 1:
                    v_high(2)
                out_copy(b - 1)
                if 1 < b < NB - 1:
                    v_high(b + 1)
                hgt_high(b)
                if b + 1 < NB:
                    v_turned(b + 1)
            out_copy(NB - 1)

        @block.vector
        def _(dve):
            chain = [0]

            def link(ins):
                chain[0] += 1
                ins.then_inc(dve_chain, 1)
                dve.wait_ge(dve_chain, chain[0])

            def lo_of(name):
                if name in NO_LOW:
                    return
                if name == "al":
                    dve.wait_ge(filled, AT[name] + 1)
                    dve.wait_ge(diag_made, 4)
                    src = bank(name)[:, 0:2 * P]
                    own = diag[:].rearrange("p h b r -> p (h b r)")
                    hi, lo = (al_s[:, half].rearrange("p h n -> p (h n)") for half in (HI, LO))
                    kept = al_kept[:].rearrange("p h n -> p (h n)")
                    dve.tensor_tensor(hi, src, own, ALU.mult).then_inc(al_masked, 1)
                    dve.tensor_tensor(kept, src, own, ALU.mult).then_inc(al_masked, 1)
                    dve.wait_ge(al_masked, 2)
                    dve.tensor_tensor(lo, kept, hi.bitcast(F32), ALU.subtract).then_inc(low, 1)
                    return
                dve.wait_ge(high, HIGHS[name])
                src, dst, by = place(name)
                hi = dst[:, HI].bitcast(F32)
                if by == 1.0:
                    dve.tensor_tensor(dst[:, LO], src, hi, ALU.subtract).then_inc(low, 1)
                else:
                    dve.scalar_tensor_tensor(dst[:, LO], src, by, hi, ALU.mult, ALU.subtract).then_inc(low, 1)

            dve.wait_ge(ld_cb, 16)
            link(dve.tensor_reduce(tiny[:, 0:1], cb[:], AX.X, ALU.max))
            link(dve.tensor_reduce(tiny[:, 1:2], cb[:], AX.X, ALU.min))
            link(dve.tensor_scalar(tiny[:, 1:2], tiny[:, 1:2], -1.0, 1e-8, ALU.mult, ALU.max))
            link(dve.tensor_tensor(tiny[:, 0:1], tiny[:, 0:1], tiny[:, 1:2], ALU.max))
            link(dve.reciprocal(tiny[:, 2:3], tiny[:, 0:1]))
            link(dve.tensor_scalar(cbn[:], cb[:], tiny[:, 2:3], None, ALU.mult))
            link(dve.tensor_tensor(thr[:, 0:7], cbn[:, 0:7], cbn[:, 1:8], ALU.add))
            link(dve.tensor_scalar(thr[:, 0:7], thr[:, 0:7], 0.5, None, ALU.mult))
            link(dve.tensor_tensor(step[:, 0:7], cbn[:, 1:8], cbn[:, 0:7], ALU.subtract))
            dve.wait_ge(la_hi, 1)
            dve.tensor_tensor(la_s[:, LO], la[:], la_s[:, HI].bitcast(F32), ALU.subtract).then_inc(la_lo, 1)
            lo_of("lbt")
            link(dve.tensor_tensor(thr[:, 2:3], thr[:, 2:3], thr[:, 1:2], ALU.max))
            link(dve.tensor_tensor(thr[:, 2:3], thr[:, 2:3], thr[:, 3:4], ALU.min))
            link(dve.tensor_tensor(thr[:, 1:2], thr[:, 1:2], thr[:, 3:4], ALU.min))
            link(dve.tensor_tensor(thr[:, 0:1], thr[:, 0:1], thr[:, 1:2], ALU.min))
            link(dve.tensor_tensor(thr[:, 4:5], thr[:, 4:5], thr[:, 5:6], ALU.min))
            link(dve.tensor_tensor(thr[:, 4:5], thr[:, 4:5], thr[:, 3:4], ALU.max))
            link(dve.tensor_tensor(thr[:, 5:6], thr[:, 5:6], thr[:, 3:4], ALU.max))
            link(dve.tensor_tensor(thr[:, 6:7], thr[:, 6:7], thr[:, 5:6], ALU.max))
            for n in USES[AT["p3_0"]:AT["c0"]]:
                lo_of(n)
            dve.wait_ge(r2_hi, 1)
            dve.tensor_tensor(r2_s[:, LO].rearrange("p k (c r) -> p k c r", r=RB), r2_four,
                              r2_s[:, HI].rearrange("p k (c r) -> p k c r", r=RB).bitcast(F32),
                              ALU.subtract).then_inc(r2_lo, 1)
            lo_of("c0")
            lo_of("c1")
            dve.wait_ge(exped, 1)
            dve.reciprocal(rscale[:], scale[:]).then_inc(rs_ready, 1)
            dve.wait_ge(rs_ready, 1)
            for k in range(KT):
                if k % 2 == 0:
                    dve.wait_ge(ld_w0[k // 2], 16)
                dve.wait_ge(high, HIGHS[f"ld{k}"])
                dve.tensor_tensor(w0[:, k], w0[:, k], ld[:, k], ALU.add).then_inc(shifted, 1)

            def level(pair, s):
                i = 6 - s
                for par in range(2):
                    n = nrm[:, 2 * pair + par].rearrange("p k n -> p (k n)")
                    a = acc[:, par].rearrange("p k n -> p (k n)")
                    if s == 0:
                        dve.wait_ge(*((q_n, 2 * pair + par) if pair + par else (q_n0, 1)))
                        if pair:
                            dve.wait_ge(q_err, par + 1)
                        dve.tensor_scalar(a, n, thr[:, i:i + 1], step[:, i:i + 1], ALU.is_gt, ALU.mult)\
                            .then_inc(q_sum, 1)
                    else:
                        dve.wait_ge(q_bias, 12 * pair + 2 * (s - 1) + par + 1)
                        b = bia[:, par].rearrange("p k n -> p (k n)")
                        dve.scalar_tensor_tensor(a, n, thr[:, i:i + 1], b, ALU.is_gt, ALU.mult).then_inc(q_sum, 1)

            def error_of(pair):
                for par in range(2):
                    g = 2 * pair + par
                    dve.wait_ge(q_sum, 14 * pair + 12 + par + 1)
                    dve.scalar_tensor_tensor(w0[:, :, g * P:(g + 1) * P], acc[:, par], cbn[:, 0:1], nrm[:, g],
                                             ALU.add, ALU.subtract).then_inc(q_err, 1)

            late = ["t2a", "t2b"]
            for pair in range(2):
                if pair == 0:
                    dve.wait_ge(shifted, KT)
                    dve.tensor_tensor(nrm[:, 0], w0[:, :, 0:P], rscale[:, :, 0:1].to_broadcast([P, KT, P]), ALU.mult)\
                        .then_inc(q_n0, 1)
                for s in range(7):
                    level(pair, s)
                    for n in late:
                        lo_of(n)
                    late = BESIDE[pair][s]
                error_of(pair)
            for n in late:
                lo_of(n)
            dve.wait_ge(q_err, G)
            link(dve.memset(vn[:].bitcast(F32), 0.0))
            dve.wait_ge(ld_lang, 16)
            dve.wait_ge(diag_made, 1)
            link(dve.tensor_copy(lang[:], lang_i[:]))
            link(dve.tensor_copy(iota[:], iota_i[:]))
            link(dve.tensor_tensor(lbias[:], iota[:, None, :].to_broadcast([P, NB, E]),
                                   lang[:, :, None].to_broadcast([P, NB, E]), ALU.is_equal))
            link(dve.tensor_scalar(lbias[:], lbias[:], LANG_BIAS, None, ALU.mult))
            for n in USES[AT["r02"]:]:
                lo_of(n)

            def v_low(b):
                l_at, a_at = v_columns(b)
                small = ps[:, SMALL[b % 2]]
                dve.wait_ge(v_hi, 2 * b + 2)
                dve.tensor_tensor(vn[:, b % 2, LO_ROW:LO_ROW + RB], small[:, l_at:l_at + RB],
                                  vn[:, b % 2, 0:RB].bitcast(F32), ALU.subtract).then_inc(v_lo, 1)
                dve.tensor_tensor(vn[:, b % 2, LO_ROW + RB:VW], small[:, a_at:a_at + RA],
                                  vn[:, b % 2, RB:V].bitcast(F32), ALU.subtract).then_inc(v_lo, 1)

            def hgt_low(b):
                dve.wait_ge(hgt_hi, b + 1)
                dve.tensor_tensor(hgt[:, LO], ps[:, HGT_BANK, 0:T], hgt[:, HI].bitcast(F32), ALU.subtract)\
                    .then_inc(hgt_lo, 1)

            def gates(b):
                small = ps[:, SMALL[b % 2], SEG - NC:SEG]
                dve.wait_ge(z_small, b + 1)
                link(dve.tensor_tensor(lg[:], small[:, 0:E], lbias[:, b], ALU.add))
                link(dve.max(top[:], lg[:]))
                dve.tensor_tensor(gw[:, 0:1], top[:, 1:2], top[:, 0:1], ALU.subtract).then_inc(gap_ready, 1)
                link(dve.max_index(top_i[:], top[:], lg[:]))
                link(dve.tensor_copy(top_f[:], top_i[:]))
                dve.wait_ge(exp_done, b + 1)
                link(dve.tensor_scalar(gw[:, 2:3], gw[:, 1:2], 1.0, None, ALU.add))
                link(dve.reciprocal(gw[:, 3:4], gw[:, 2:3]))
                link(dve.tensor_tensor(gw[:, 4:5], gw[:, 1:2], gw[:, 3:4], ALU.mult))
                link(dve.tensor_scalar(gate[:, 0], iota[:], top_f[:, 0:1], gw[:, 3:4], ALU.is_equal, ALU.mult))
                link(dve.tensor_scalar(gate[:, 1], iota[:], top_f[:, 1:2], gw[:, 4:5], ALU.is_equal, ALU.mult))
                link(dve.tensor_tensor(gate[:, 2], gate[:, 0], gate[:, 1], ALU.add))
                if b >= 2:
                    dve.wait_ge(hgt_up, b - 1)
                dve.tensor_tensor(hg[:, b % 2].rearrange("p (e r) -> p e r", e=E),
                                  small[:, E:NC].rearrange("p (e r) -> p e r", e=E),
                                  gate[:, 2, :, None].to_broadcast([P, E, RE]), ALU.mult).then_inc(hg_ready, 1)

            v_low(0)
            v_low(1)
            for b in range(NB):
                gates(b)
                if 1 <= b < NB - 1:
                    v_low(b + 1)
                hgt_low(b)

        @block.tensor
        def _(pe):
            def use(name):
                if AT[name] >= 8:
                    before = USES[AT[name] - 8]
                    if before in NO_LOW:
                        pe.wait_ge(high, HIGHS[before])
                    else:
                        pe.wait_ge(low, LOWS[before])

            def split(name):
                pe.wait_ge(low, LOWS[name])

            def product(dst, terms, first=True, last=True):
                n = 0
                for lhs, rhs in terms:
                    for a, b in PASSES:
                        mm = pe.matmul(dst, lhs(a), rhs(b), start=(first and n == 0),
                                       stop=(last and n == 3 * len(terms) - 1))
                        n += 1
                return mm

            pe.wait_ge(made, 2)
            for k in range(WARM_UPS):
                pe.transpose(bank("c1")[:, 0:P], ident[:], ident[:])
            use("lbt")
            pe.wait_ge(ld_lb, 16)
            for k in range(KT):
                mm = pe.transpose(bank("lbt")[0:RL0, k * P:(k + 1) * P], lb[:, k], ident[:])
            mm.then_inc(filled, 1)
            for k in range(WARM_AGAIN):
                pe.transpose(bank("c1")[:, 0:P], ident[:], ident[:])
            for half in range(2):
                pe.wait_ge(ld_w3[half], 16)
                for m in range(KT):
                    use(f"p3_{m}")
                    for k in sorted((2 * half, 2 * half + 1), key=lambda k: k == m):
                        if k == m:
                            pe.wait_ge(eye3, k + 1)
                        mm = pe.transpose(bank(f"p3_{m}")[:, k * P:(k + 1) * P], w3[:, k, m * P:(m + 1) * P], ident[:])
                    if half:
                        mm.then_inc(filled, 1)
            pe.wait_ge(ld_wr, 16)
            pe.wait_ge(ld_a3, 16)
            for j in range(2):
                use(f"c{j}")
                for i in range(2):
                    k = 2 * j + i
                    pe.transpose(bank(f"c{j}")[:, i * NC:i * NC + E], wr[:, k * P:(k + 1) * P], ident[0:E, 0:E])
                    mm = pe.transpose(bank(f"c{j}")[:, i * NC + E:(i + 1) * NC], a3[:, k * P:(k + 1) * P], ident[:])
                mm.then_inc(filled, 1)

            def w2_cols(m, i):
                return lambda s: pc[:, s, m, QW + i * P:QW + (i + 1) * P]

            def p3c(m, h):
                return lambda s: pc[:, s, m, h * QP:(h + 1) * QP]

            def qcv(m, a, b):
                return lambda s: qc[:, s, m, a:b]

            def ld_block(k):
                use(f"ld{k}")
                product(bank(f"ld{k}"), [(lambda s: lbt_s[:, s, k * P:(k + 1) * P], lambda s: la_s[:, s])])\
                    .then_inc(filled, 1)

            split("lbt")
            pe.wait_ge(la_lo, 1)
            for k in range(KT):
                ld_block(k)
            pe.wait_ge(r2_lo, 1)
            for h in range(2):
                name = "t2" + "ab"[h]
                use(name)
                split(("p3_3", "c1")[h])
                product(bank(name)[:, 0:QP], [(lambda s, m=m: r2_s[:, s, m], p3c(m, h)) for m in range(KT)])\
                    .then_inc(filled, 1)

            def qc_block(i, h):
                name = f"qc{i}" + "ab"[h]
                use(name)
                for m in range(KT):
                    if i == h == 0:
                        pe.wait_ge(w2_low, m + 1)
                    mm = product(bank(name)[:, 0:QP], [(w2_cols(m, i), p3c(m, h))], m == 0, m == KT - 1)
                mm.then_inc(filled, 1)

            for i in range(KT):
                qc_block(i, 0)
                qc_block(i, 1)
            use("al")
            pe.wait_ge(l2_lo, NB // BG)
            pe.wait_ge(a1_lo, 1)
            for q in range(NB // BG):
                mm = product(bank("al")[:, q * P:(q + 1) * P],
                             [(lambda s, k=k, q=q: l2_cols[:, s, k, q], lambda s, k=k: a1_s[:, s, k])
                              for k in range(KT)])
            mm.then_inc(filled, 1)
            use("b1t")
            pe.wait_ge(ld_b1, 16 * NB)
            for k in range(KT):
                mm = pe.transpose(bank("b1t")[:, k * P:(k + 1) * P], b1[:, k * P:(k + 1) * P], ident[:])
            mm.then_inc(filled, 1)
            use("b3t")
            pe.wait_ge(ld_b3, 16 * KT)
            for k in range(KT):
                mm = pe.transpose(bank("b3t")[:, k * P:(k + 1) * P], b3[:, k].rearrange("p e r -> p (e r)"), ident[:])
            mm.then_inc(filled, 1)
            for h in range(2):
                a, b = h * QP, (h + 1) * QP
                use("t1" + "ab"[h])
                split("qc3" + "ab"[h])
                product(bank("t1" + "ab"[h])[:, 0:QP],
                        [(lambda s, m=m: a1_s[:, s, m], qcv(m, a, b)) for m in range(KT)], last=False)
            split("t2b")
            split("al")
            for h in range(2):
                a, b = h * QP, (h + 1) * QP
                product(bank("t1" + "ab"[h])[:, 0:QP],
                        [(lambda s, q=q: al_s[:, s, q], lambda s, a=a, b=b: t2[:, s, a:b]) for q in range(2)],
                        first=False).then_inc(filled, 1)

            def r_block(g):
                pe.wait_ge(w0_lo, g + 1)
                for c in range(3):
                    use(f"r{g}{c}")
                    if g == 0 and c == 1:
                        split("b1t")
                    product(bank(f"r{g}{c}")[:, 0:RP],
                            [(lambda s, m=m: w0_s[:, s, m, g * P:(g + 1) * P], qcv(m, c * RP, (c + 1) * RP))
                             for m in range(KT)]).then_inc(filled, 1)

            r_block(0)
            r_block(1)
            for b in range(NB):
                use(f"x{b}")
                if b % 4 == 0:
                    pe.wait_ge(ld_x[b // 4], 16)
                src = (x_a, x_b)[b // 4]
                for k in range(KT):
                    mm = pe.transpose(bank(f"x{b}")[:, k * P:(k + 1) * P], src[:, b % 4, k * P:(k + 1) * P], ident[:])
                mm.then_inc(filled, 1)
            r_block(2)
            r_block(3)

            row = 2 * KT * XW

            def small_cols(b, k, s):
                base = pc[:, s, k, QW - SEG:QW]
                there = SEG + b // BG * GW + b % BG * RB
                return bass.AP(base.tensor, base.offset, [[row, P], [there, 2], [1, SEG]])

            def small(b, ks):
                if b >= 2 and 0 in ks:
                    pe.wait_ge(hg_ready, b - 1)
                for k in ks:
                    for n, (u, w) in enumerate(PASSES):
                        mm = pe.matmul(ps[:, SMALL[b % 2], 0:2 * SEG], xt[:, u, b, k], small_cols(b, k, w),
                                       start=(k == 0 and n == 0), stop=(k == KT - 1 and n == 2))
                if KT - 1 in ks:
                    mm.then_inc(small_done, 1)

            def main(b, ks):
                if b >= 3 and 0 in ks:
                    pe.wait_ge(out_copied, b - 3 + len(main_parts(b)))
                for bk, a, e in main_parts(b):
                    for k in ks:
                        for n, (u, w) in enumerate(PASSES):
                            pe.matmul(ps[:, bk, 0:e - a], xt[:, u, b, k], pc[:, w, k, a:e],
                                      start=(k == 0 and n == 0), stop=False, skip_group_check=True)

            def turn_v(b):
                pe.wait_ge(v_lo, 2 * b + 2)
                if b >= 1:
                    pe.wait_ge(vt_copied, b)
                pe.transpose(ps[0:VW, VT_BANK, 0:T].bitcast(F32), vn[:, b % 2, 0:VW].bitcast(F32), ident[:])\
                    .then_inc(vt_up, 1)

            def add_v(b, dst, a, e, stop):
                s = b % NS
                pe.matmul(dst, vt[0:VW, b % 2], s_hi[:, s, a:e], start=False, stop=False, skip_group_check=True)
                return pe.matmul(dst, vt[0:V, b % 2], s_lo[:, s, a:e], start=False, stop=stop,
                                 skip_group_check=True)

            def add_v_small(b):
                pe.wait_ge(vt_copied, b + 1)
                pe.wait_ge(s_loaded[b % NS], 48 * (b // NS + 2))
                add_v(b, ps[:, SMALL[b % 2], SEG - NC:SEG], D, QW, True).then_inc(z_small, 1)

            def add_v_main(b):
                for bk, a, e in main_parts(b):
                    mm = add_v(b, ps[:, bk, 0:e - a], a, e, False)
                mm.then_inc(z_main, 1)

            def turn_hg(b):
                pe.wait_ge(hg_ready, b + 1)
                if b >= 1:
                    pe.wait_ge(hgt_lo, b)
                pe.transpose(ps[:, HGT_BANK, 0:T], hg[:, b % 2], ident[:]).then_inc(hgt_up, 1)

            def add_experts(b):
                pe.wait_ge(hgt_lo, b + 1)
                for bk, a, e in main_parts(b):
                    for n, (u, w) in enumerate(PASSES):
                        mm = pe.matmul(ps[:, bk, 0:e - a], hgt[:, u], b3t[:, w, a:e], start=False, stop=(n == 2),
                                       skip_group_check=True)
                    mm.then_inc(main_done, 1)

            split(f"r{G - 2}2")
            small(0, range(KT - 1))
            main(0, range(KT - 1))
            split(f"r{G - 1}2")
            small(0, [KT - 1])
            small(1, range(KT))
            turn_v(0)
            main(0, [KT - 1])
            add_v_small(0)
            turn_v(1)
            main(1, [0])
            add_v_main(0)
            add_v_small(1)
            main(1, [1, 2, 3])
            turn_hg(0)
            add_v_main(1)
            small(2, range(KT))
            add_experts(0)
            for b in range(2, NB - 2):
                if b > 2:
                    small(b, range(KT))
                main(b, [0, 1])
                turn_hg(b - 1)
                turn_v(b)
                main(b, [2])
                add_v_small(b)
                add_experts(b - 1)
                main(b, [3])
                add_v_main(b)
            b, z = NB - 2, NB - 1
            small(b, range(KT))
            main(b, [0])
            turn_hg(b - 1)
            turn_v(b)
            main(b, [1])
            add_v_small(b)
            add_experts(b - 1)
            small(z, range(KT))
            main(b, [2])
            turn_hg(b)
            turn_v(z)
            main(b, [3])
            add_v_small(z)
            add_v_main(b)
            add_experts(b)
            main(z, [0, 1, 2])
            turn_hg(z)
            main(z, [3])
            add_v_main(z)
            add_experts(z)


_INS = ["x", "condB_codebook", "itok_B_3_7", "itok_B_0_2", "itok_B_0_7", "L0_cond_weight", "L0_cond_scale_log",
        "L0_cond_lora_A", "L0_cond_lora_B", "L1_cond_A", "L1_cond_B", "L2_cond_W", "L2_cond_lora_A",
        "L2_cond_lora_B_w", "L3_cond_W", "L3_cond_Wr", "L3_cond_A", "L3_cond_B"]


def kernel(**inputs):
    import numpy as np
    import concourse.bacc as bacc
    from concourse.bass_utils import run_bass_kernel_spmd

    nc = bacc.Bacc("TRN2", target_bir_lowering=False, num_devices=1)
    arrays, args = {}, []
    for name in _INS:
        a = np.ascontiguousarray(inputs[name])
        arrays[f"in_{name}"] = a
        args.append(nc.dram_tensor(f"in_{name}", a.shape, mybir.dt.from_np(a.dtype), kind="ExternalInput").ap())
    out = nc.dram_tensor("out_dram", inputs["x"].shape, F32, kind="ExternalOutput").ap()
    layer_chain(nc, *args, out)
    r = run_bass_kernel_spmd(nc, [arrays], core_ids=[0])
    return r.results[0]["out_dram"]
```

```python
from contextlib import ExitStack

import concourse.bass as bass
from concourse import mybir

F32 = mybir.dt.float32
F32R = mybir.dt.float32r
I32 = mybir.dt.int32
U32 = mybir.dt.uint32
ALU = mybir.AluOpType
ACT = mybir.ActivationFunctionType
AX = mybir.AxisListType

P = 128
HI, LO = 0, 1
PASSES = ((HI, HI), (HI, LO), (LO, HI))


def layer_chain(nc, x, codebook, adapter_id, labeler_id, language_id, W0, scale_log, LA0, LB0, A1, B1, W2, L2, R2,
                W3, Wr, A3, B3, out):
    NB, T, D = x.shape
    KT = D // P
    G = KT
    RL0 = LA0.shape[0]
    RA = A1.shape[2]
    RB = L2.shape[2]
    E, RE = A3.shape[0], A3.shape[1]
    NC = E + E * RE
    V = RB + RA
    QW = D + NC
    RW = QW + NB * V
    QP = QW // 2
    RP = RW // 3
    XW = QW + D
    SW = 2 * NC
    NCB = codebook.shape[0]
    assert (T, D, NC, V, NB * RA, NCB, E) == (P, 512, 136, 48, P, 8, 8) and RW % 3 == 0
    LORA0_SCALE, L2_SCALE, L3_SCALE, LANG_BIAS = 0.5, 0.5, 2.0, 5.0
    LO_ROW = 64
    VW = LO_ROW + V
    NS, NOUT = 3, 3
    WARM_UPS, WARM_AGAIN = 13, 15

    ctx = ExitStack()
    with ctx:
        at = [(nc.sbuf_base + 63) // 64 * 64]

        def put(name, shape, dt, offset):
            return nc.alloc_sbuf_tensor_at(name, shape, dt, offset=offset)

        def sb(name, shape, dt=F32):
            n = 4
            for s in shape[1:]:
                n *= s
            offset = at[0]
            at[0] += (n + 63) // 64 * 64
            assert at[0] <= nc.sbuf_top, (name, at[0], nc.sbuf_top)
            return put(name, shape, dt, offset), offset

        w0, w0_at = sb("w0", [P, KT, D])
        w2, w2_at = sb("w2", [P, KT, D])
        w3, w3_at = sb("w3", [P, KT, D])
        x_a, _ = sb("x_first_half", [P, NB // 2, D])
        x_b = put("x_second_half", [P, NB // 2, D], F32, w3_at)
        early_at = at[0]
        lb, _ = sb("lb", [P, KT, RL0])
        la, _ = sb("la", [RL0, D])
        la_s, _ = sb("la_split", [RL0, 2, D], F32R)
        lbt_s, _ = sb("lbt_split", [RL0, 2, D], F32R)
        a3, _ = sb("a3", [P, D])
        b1, _ = sb("b1", [P, D])
        l2, _ = sb("l2", [P, KT, NB, RB])
        early_end = at[0]
        r2, _ = sb("r2", [P, KT, RB])
        b3, _ = sb("b3", [P, KT, E, RE])
        xt, xt_at = sb("xt_split", [P, 2, NB, KT, T], F32R)
        kb = D * 4
        r2_s = put("r2_split", [P, 2, KT, RB], F32R, xt_at + kb)
        a1 = put("a1", [P, KT, NB, RA], F32, xt_at + 3 * kb)
        a1_s = put("a1_split", [P, 2, KT, P], F32R, xt_at + 4 * kb)
        wr = put("wr", [E, D], F32, xt_at + 8 * kb)
        al = put("al", [P, NB, RB], F32, xt_at + 6 * kb)
        al_s = put("al_split", [RB, 2, P], F32R, xt_at + 7 * kb)
        w0_s, _ = sb("w0_split", [P, 2, KT, D], F32R)
        pc, _ = sb("p3c_w2_then_r", [P, 2, KT, XW], F32R)
        qc, _ = sb("qc_split", [P, 2, KT, RW], F32R)
        b3t, _ = sb("b3t_split", [P, 2, D], F32R)
        t1 = put("t1_split", [P, 2, QW], F32R, w2_at)
        t2, _ = sb("t2_split", [RB, 2, QW], F32R)
        s_hi = put("s_hi", [VW, NS, QW], F32R, early_at)
        s_lo = put("s_lo", [V, NS, QW], F32R, early_at + NS * QW * 4)
        assert early_end - early_at >= 2 * NS * QW * 4, (early_end - early_at)
        outs = put("out_rows", [P, NOUT, D], F32, w0_at)
        ld, _ = sb("ld", [P, KT, D])
        nrm, _ = sb("normalized", [P, G, KT, P])
        acc, acc_at = sb("level_sum", [P, 2, KT, P])
        bia, _ = sb("level_biased", [P, 2, KT, P])
        ident, _ = sb("ident", [P, P])
        iota_i, _ = sb("iota_i", [P, E], I32)
        iota, _ = sb("iota", [P, E])
        ids_a, _ = sb("ids_adapter", [1, NB], I32)
        ids_l, _ = sb("ids_labeler", [1, NB], I32)
        lang_i, _ = sb("lang_i", [P, NB], I32)
        lang, _ = sb("lang", [P, NB])
        lbias, _ = sb("lang_bias", [P, NB, E])
        cb, _ = sb("cb", [P, NCB])
        cbn, _ = sb("cbn", [P, NCB])
        thr, _ = sb("thr", [P, NCB])
        step, _ = sb("step", [P, NCB])
        tiny, _ = sb("tiny", [P, 4])
        slog, _ = sb("slog", [P, KT, G])
        scale, _ = sb("scale", [P, KT, G])
        rscale, _ = sb("rscale", [P, KT, G])
        vn = put("v_rows", [P, 2, P], F32R, acc_at)
        vt = put("v_cols", [P, 2, T], F32R, acc_at + 2 * P * 4)
        lg, _ = sb("logits", [P, E])
        top, _ = sb("top", [P, 8])
        top_i, _ = sb("top_i", [P, 8], U32)
        top_f, _ = sb("top_f", [P, 8])
        gw, _ = sb("gate_weights", [P, 8])
        gate, _ = sb("gate", [P, 3, E])
        hg = put("h_gated", [P, 2, E * RE], F32, acc_at + 4 * P * 4)
        hgt = put("hgt_split", [P, 2, T], F32R, acc_at + 6 * P * 4)

        ps = ctx.enter_context(nc.psum_tensor("ps", [P, 8, 512], F32))

        def sem(name):
            return ctx.enter_context(nc.semaphore(name))

        ld_ids, ld_lang, ld_cb, ld_scale, ld_lb, ld_la = (
            sem(f"loaded_{n}") for n in ("ids", "lang", "cb", "scale", "lb", "la"))
        ld_w3 = [sem(f"loaded_w3_{i}") for i in range(2)]
        ld_w2 = [sem(f"loaded_w2_{i}") for i in range(2)]
        ld_w0 = [sem(f"loaded_w0_{i}") for i in range(2)]
        ld_wr, ld_a3, ld_b3, ld_r2, ld_b1, ld_l2, ld_a1 = (
            sem(f"loaded_{n}") for n in ("wr", "a3", "b3", "r2", "b1", "l2", "a1"))
        ld_x = [sem(f"loaded_x_{i}") for i in range(2)]
        s_loaded = [sem(f"s_loaded_{i}") for i in range(NS)]
        stored = [sem(f"stored_{i}") for i in range(NOUT)]
        made = sem("constants_made")
        s_zeroed = sem("s_rows_zeroed")
        eye3, eye2 = sem("w3_plus_identity"), sem("w2_plus_identity")
        shifted, eye_ld = sem("w0_plus_ld"), sem("ld_plus_identity")
        counted = sem("iota_made")
        w2_hi, w2_low = sem("w2_hi"), sem("w2_lo")
        la_hi, la_lo = sem("la_hi"), sem("la_lo")
        a1_hi, a1_lo = sem("a1_hi"), sem("a1_lo")
        l2_hi, l2_lo = sem("l2_hi"), sem("l2_lo")
        r2_hi, r2_lo = sem("r2_hi"), sem("r2_lo")
        filled, high, low = sem("bank_filled"), sem("bank_high"), sem("bank_low")
        exped, dve_chain = sem("scale_exp"), sem("dve_chain")
        rs_ready, q_n0 = sem("rscale_ready"), sem("quant_first_normal")
        q_n, q_sum, q_bias, q_err, q_fin = (sem(f"quant_{n}") for n in ("normal", "sum", "bias", "err", "fin"))
        w0_hi, w0_lo = sem("w0_hi"), sem("w0_lo")
        small_done, v_hi, v_lo, vt_up, vt_copied, z_small, z_main = (
            sem(n) for n in ("small_done", "v_hi", "v_lo", "v_turned", "v_copied", "z_small", "z_main"))
        gap_ready, exp_done, hg_ready, hgt_up, hgt_hi, hgt_lo, main_done, out_copied = (
            sem(n) for n in ("gap_ready", "exp_done", "hg_ready", "hg_turned", "hgt_hi", "hgt_lo", "main_done",
                             "out_copied"))

        USES = (["lbt"] + [f"p3_{i}" for i in range(KT)] + ["c0", "c1"] + [f"ld{i}" for i in range(KT)] + ["t2a", "t2b"]
                + [f"qc{i}{h}" for i in range(KT) for h in "ab"]
                + ["al", "b1t", "alt", "t1a", "t1b"] + [f"r{g}{c}" for g in range(G // 2) for c in range(3)]
                + [f"x{b}" for b in range(NB)] + ["b3t"] + [f"r{g}{c}" for g in range(G // 2, G) for c in range(3)])
        AT = {n: i for i, n in enumerate(USES)}
        NO_LOW = [f"ld{i}" for i in range(KT)] + ["al"]
        HIGHS = {n: i + 1 for i, n in enumerate(USES)}
        LOWS = {n: len([m for m in USES[:i + 1] if m not in NO_LOW]) for i, n in enumerate(USES)}

        def bank(name):
            return ps[:, AT[name] % 8]

        def place(name):
            u = ps[:, AT[name] % 8]
            if name == "lbt":
                return u[0:RL0, :], lbt_s[:, :, :], LORA0_SCALE
            if name[0] == "c":
                j = 2 * int(name[1])
                return (u[:, 0:2 * NC].rearrange("p (k n) -> p k n", k=2), pc[:, :, j:j + 2, D:QW], 1.0)
            if name.startswith("p3"):
                return u, pc[:, :, int(name[3]), 0:D], 1.0
            if name.startswith("qc"):
                h = "ab".index(name[3])
                return u[:, 0:QP], qc[:, :, int(name[2]), h * QP:(h + 1) * QP], 1.0
            if name[0] == "x":
                return u.rearrange("p (k t) -> p k t", k=KT), xt[:, :, int(name[1])], 1.0
            if name == "b1t":
                return u.rearrange("p (k b r) -> p k b r", k=KT, b=NB), own_cols[:, :, :, :, RB:V], 1.0
            if name == "alt":
                return u[0:RB, 0:P], al_s[:, :, :], 1.0
            if name == "b3t":
                return u, b3t[:, :, :], L3_SCALE
            if name[0] == "t":
                h = "ab".index(name[2])
                if name[1] == "1":
                    return u[:, 0:QP], t1[:, :, h * QP:(h + 1) * QP], 1.0
                return u[0:RB, 0:QP], t2[:, :, h * QP:(h + 1) * QP], L2_SCALE
            if name[0] == "r":
                c = int(name[2])
                return u[:, 0:RP], pc[:, :, int(name[1]), c * RP:(c + 1) * RP], 1.0
            raise KeyError(name)

        after = [(len(USES) + i) % 8 for i in range(8)]
        MAIN, SMALL, VT_BANK, HGT_BANK = after[0:2] + after[5:6], after[2:4], after[6], after[7]
        HIGH_AT = (1, 4)
        BESIDE = [[["qc0a", "qc0b"], ["qc1a"], ["qc1b"], ["qc2a"], ["qc2b"], ["qc3a"], ["qc3b", "al", "b1t", "alt"]],
                  [[], [], [], ["t1a"], ["t1b"], ["r00"], ["r01"]]]
        own_cols = qc[:, :, :, QW:RW].rearrange("p s k (b n) -> p s k b n", n=V)
        l2_cols = own_cols[:, :, :, :, 0:RB]

        def main_parts(b):
            if b < NB - 1:
                return [(MAIN[b % 3], 0, D)]
            return [(MAIN[b % 3], 0, D // 2), (MAIN[(b + 1) % 3], D // 2, D)]

        def rows(w):
            return w.rearrange("(k p) n -> p k n", p=P)

        block = ctx.enter_context(nc.Block())

        @block.sync
        def _(sp):
            sp.dma_start(cb[:], codebook.partition_broadcast(P)).then_inc(ld_cb, 16)
            sp.dma_start(lb[:], rows(LB0)).then_inc(ld_lb, 16)
            sp.dma_start(la[:], LA0).then_inc(ld_la, 16)
            for i in range(2):
                sp.dma_start(w3[:, 2 * i:2 * i + 2], rows(W3)[:, 2 * i:2 * i + 2]).then_inc(ld_w3[i], 16)
            sp.dma_start(wr[:], Wr).then_inc(ld_wr, 16)
            sp.dma_start(a3[:], A3.rearrange("e r d -> (e r) d")).then_inc(ld_a3, 16)
            sp.dma_start(ids_a[:], adapter_id.rearrange("(a n) -> a n", a=1)).then_inc(ld_ids, 16)
            sp.dma_start(ids_l[:], labeler_id.rearrange("(a n) -> a n", a=1)).then_inc(ld_ids, 16)
            sp.dma_start(r2[:], rows(R2)).then_inc(ld_r2, 16)
            for i in range(2):
                sp.dma_start(w2[:, 2 * i:2 * i + 2], rows(W2)[:, 2 * i:2 * i + 2]).then_inc(ld_w2[i], 16)
            sp.dma_start(slog[:], scale_log.rearrange("(k p) g a -> p k (g a)", p=P)).then_inc(ld_scale, 16)
            for i in range(2):
                sp.dma_start(w0[:, 2 * i:2 * i + 2], rows(W0)[:, 2 * i:2 * i + 2]).then_inc(ld_w0[i], 16)
            sp.wait_ge(ld_ids, 32)
            labeler = [sp.value_load(ids_l[0:1, b:b + 1], min_val=0, max_val=L2.shape[0] - 1) for b in range(NB)]
            for b in range(NB):
                sp.dma_start(l2[:, :, b, :], L2[bass.ds(labeler[b], 1)].rearrange("e (k p) r -> p (e k) r", p=P))\
                  .then_inc(ld_l2, 16)
            adapter = [sp.value_load(ids_a[0:1, b:b + 1], min_val=0, max_val=A1.shape[0] - 1) for b in range(NB)]
            for b in range(NB):
                sp.dma_start(a1[:, :, b, :], A1[bass.ds(adapter[b], 1)].rearrange("e (k p) r -> p (e k) r", p=P))\
                  .then_inc(ld_a1, 16)
            for b in range(NB):
                sp.dma_start(b1[b * RA:(b + 1) * RA, :], B1[bass.ds(adapter[b], 1)].rearrange("e r d -> (e r) d"))\
                  .then_inc(ld_b1, 16)
            for k in range(KT):
                sp.dma_start(b3[:, k], B3.rearrange("e (k p) r -> k p e r", p=P)[k]).then_inc(ld_b3, 16)
            sp.dma_start(x_a[:], x[0:NB // 2].rearrange("b t d -> t b d")).then_inc(ld_x[0], 16)
            sp.wait_ge(filled, AT[f"p3_{KT - 1}"] + 1)
            sp.dma_start(x_b[:], x[NB // 2:NB].rearrange("b t d -> t b d")).then_inc(ld_x[1], 16)
            sp.dma_start(lang_i[:], language_id.partition_broadcast(P)).then_inc(ld_lang, 16)

            sp.wait_ge(low, LOWS["b1t"])
            for s in range(NS):
                for dst, half in ((s_hi[0:RB, s], HI), (s_hi[LO_ROW:LO_ROW + RB, s], HI), (s_lo[0:RB, s], LO)):
                    sp.dma_start(dst.bitcast(F32), t2[0:RB, half].bitcast(F32)).then_inc(s_loaded[s], 16)
            sp.wait_ge(low, LOWS["t1b"])
            sp.wait_ge(s_zeroed, 1)
            for b in range(NB + NOUT):
                if b < NB:
                    if b >= NS:
                        sp.wait_ge(z_main, b - NS + 1)
                    s = b % NS
                    for dst, half in ((s_hi[RB:V, s], HI), (s_hi[LO_ROW + RB:VW, s], HI), (s_lo[RB:V, s], LO)):
                        sp.dma_start(dst.bitcast(F32), t1[b * RA:(b + 1) * RA, half].bitcast(F32)).then_inc(s_loaded[s], 16)
                o = b - NOUT
                if o >= 0:
                    for i, (_, a, e) in enumerate(main_parts(o)):
                        sp.wait_ge(out_copied, o + 1 + i)
                        sp.dma_start(out[o, :, a:e], outs[:, o % NOUT, a:e]).then_inc(stored[o % NOUT], 16)
            for s in range(NOUT):
                sp.wait_ge(stored[s], 16 * sum(len(main_parts(b)) for b in range(s, NB, NOUT)))

        @block.gpsimd
        def _(pool):
            pool.memset(ident[:], 0.0).then_inc(made, 1)
            pool.wait_ge(made, 1)
            pool.affine_select(out=ident[:], in_=ident[:], compare_op=ALU.not_equal, fill=1.0, base=0,
                               pattern=[[-1, P]], channel_multiplier=1).then_inc(made, 1)
            pool.wait_ge(made, 2)
            for k in range(KT):
                if k % 2 == 0:
                    pool.wait_ge(ld_w3[k // 2], 16)
                pool.tensor_tensor(w3[:, k, k * P:(k + 1) * P], w3[:, k, k * P:(k + 1) * P], ident[:], ALU.add)\
                    .then_inc(eye3, 1)
            pool.iota(iota_i[:], [[1, E]], base=0, channel_multiplier=0).then_inc(counted, 1)
            for k in range(KT):
                if k % 2 == 0:
                    pool.wait_ge(ld_w2[k // 2], 16)
                pool.tensor_tensor(w2[:, k, k * P:(k + 1) * P], w2[:, k, k * P:(k + 1) * P], ident[:], ALU.add)\
                    .then_inc(eye2, 1)
            for k in range(KT):
                pool.wait_ge(w2_hi, k + 1)
                pool.tensor_tensor(pc[:, LO, k, QW:XW], w2[:, k], pc[:, HI, k, QW:XW].bitcast(F32), ALU.subtract)\
                    .then_inc(w2_low, 1)
            pool.wait_ge(rs_ready, 1)
            pool.wait_ge(shifted, KT)
            for g in range(1, G):
                pool.tensor_tensor(nrm[:, g], w0[:, :, g * P:(g + 1) * P],
                                   rscale[:, :, g:g + 1].to_broadcast([P, KT, P]), ALU.mult).then_inc(q_n, 1)

            def add_back(g):
                cols = w0[:, :, g * P:(g + 1) * P]
                pool.wait_ge(q_err, g + 1)
                pool.tensor_tensor(cols, cols, nrm[:, g], ALU.add).then_inc(q_fin, 1)

            def finish(g):
                cols = w0[:, :, g * P:(g + 1) * P]
                pool.wait_ge(q_fin, 3 * g + 1)
                pool.tensor_tensor(cols, cols, scale[:, :, g:g + 1].to_broadcast([P, KT, P]), ALU.mult)\
                    .then_inc(q_fin, 1)
                pool.wait_ge(q_fin, 3 * g + 2)
                if g == 0:
                    pool.wait_ge(eye_ld, KT)
                pool.tensor_tensor(cols, cols, ld[:, :, g * P:(g + 1) * P], ALU.add).then_inc(q_fin, 1)

            def w0_low(g):
                pool.wait_ge(w0_hi, g + 1)
                cols = slice(g * P, (g + 1) * P)
                pool.tensor_tensor(w0_s[:, LO, :, cols], w0[:, :, cols], w0_s[:, HI, :, cols].bitcast(F32),
                                   ALU.subtract).then_inc(w0_lo, 1)

            for k in range(KT):
                pool.wait_ge(shifted, k + 1)
                pool.tensor_tensor(ld[:, k, k * P:(k + 1) * P], ld[:, k, k * P:(k + 1) * P], ident[:], ALU.add)\
                    .then_inc(eye_ld, 1)

            pool.wait_ge(l2_hi, 1)
            pool.tensor_tensor(l2_cols[:, LO], l2[:], l2_cols[:, HI].bitcast(F32), ALU.subtract).then_inc(l2_lo, 1)
            pool.wait_ge(a1_hi, 1)
            pool.tensor_tensor(a1_s[:, LO].rearrange("p k n -> p (k n)"),
                               a1[:].rearrange("p k b r -> p (k b r)"),
                               a1_s[:, HI].rearrange("p k n -> p (k n)").bitcast(F32), ALU.subtract)\
                .then_inc(a1_lo, 1)
            for g in (0, 2):
                add_back(g)
                finish(g)
                add_back(g + 1)
                w0_low(g)
                finish(g + 1)
                w0_low(g + 1)
            pool.wait_ge(low, LOWS["b1t"])
            pool.wait_ge(w0_lo, G)
            pool.memset(s_hi[RB:LO_ROW].bitcast(F32), 0.0).then_inc(s_zeroed, 1)

        @block.scalar
        def _(act):
            def hi_of(name):
                act.wait_ge(filled, AT[name] + 1)
                if name in NO_LOW:
                    dst = al[:].rearrange("p b r -> p (b r)") if name == "al" else ld[:, int(name[2])]
                    act.activation(dst, bank(name)[:, 0:dst.shape[1]], ACT.Copy).then_inc(high, 1)
                else:
                    src, dst, by = place(name)
                    act.activation(dst[:, HI], src, ACT.Copy, scale=by).then_inc(high, 1)

            def add_step(pair, s):
                for par in range(2):
                    act.wait_ge(q_sum, 14 * pair + 2 * s + par + 1)
                    act.activation(bia[:, par], acc[:, par], ACT.Identity, bias=step[:, 5 - s:6 - s])\
                        .then_inc(q_bias, 1)

            def w0_high(g):
                act.wait_ge(q_fin, 3 * g + 3)
                act.activation(w0_s[:, HI, :, g * P:(g + 1) * P], w0[:, :, g * P:(g + 1) * P], ACT.Copy)\
                    .then_inc(w0_hi, 1)

            act.wait_ge(ld_la, 16)
            act.activation(la_s[:, HI], la[:], ACT.Copy).then_inc(la_hi, 1)
            for n in USES[:AT["c0"]]:
                hi_of(n)
            act.wait_ge(ld_r2, 16)
            act.activation(r2_s[:, HI], r2[:], ACT.Copy).then_inc(r2_hi, 1)
            hi_of("c0")
            hi_of("c1")
            for k in range(KT):
                act.wait_ge(eye2, k + 1)
                act.activation(pc[:, HI, k, QW:XW], w2[:, k], ACT.Copy).then_inc(w2_hi, 1)
                hi_of(f"ld{k}")
                if k == 1:
                    act.wait_ge(ld_scale, 16)
                    act.activation(scale[:], slog[:], ACT.Exp).then_inc(exped, 1)
            for n in ["t2a", "t2b"]:
                hi_of(n)
            act.wait_ge(ld_l2, 16 * NB)
            act.activation(l2_cols[:, HI], l2[:], ACT.Copy).then_inc(l2_hi, 1)
            for pair in range(2):
                for s in range(7):
                    if pair == 1 and s in HIGH_AT:
                        w0_high(HIGH_AT.index(s))
                    if s < 6:
                        add_step(pair, s)
                    if (pair, s) == (0, 3):
                        act.wait_ge(ld_a1, 16 * NB)
                        act.activation(a1_s[:, HI], a1[:].rearrange("p k b r -> p k (b r)"), ACT.Copy)\
                            .then_inc(a1_hi, 1)
                    for n in BESIDE[pair][s]:
                        hi_of(n)
            for n in USES[AT["r02"]:]:
                hi_of(n)
                if n == "r10":
                    w0_high(2)
                if n == "x7":
                    w0_high(3)

            def v_high(b):
                act.wait_ge(small_done, b + 1)
                if b >= 2:
                    act.wait_ge(vt_up, b - 1)
                act.activation(vn[:, b % 2, 0:V], ps[:, SMALL[b % 2], SW - V:SW], ACT.Copy).then_inc(v_hi, 1)

            def v_turned(b):
                act.wait_ge(vt_up, b + 1)
                if b >= 2:
                    act.wait_ge(z_main, b - 1)
                act.activation(vt[0:VW, b % 2], ps[0:VW, VT_BANK, 0:T], ACT.Copy).then_inc(vt_copied, 1)

            def gate_exp(b):
                act.wait_ge(gap_ready, b + 1)
                act.activation(gw[:, 1:2], gw[:, 0:1], ACT.Exp).then_inc(exp_done, 1)

            def hgt_high(b):
                act.wait_ge(hgt_up, b + 1)
                if b >= 1:
                    act.wait_ge(main_done, b)
                act.activation(hgt[:, HI], ps[:, HGT_BANK, 0:T], ACT.Copy).then_inc(hgt_hi, 1)

            def out_copy(b):
                if b >= NOUT:
                    act.wait_ge(stored[b % NOUT], 16 * (b // NOUT))
                for i, (bk, a, e) in enumerate(main_parts(b)):
                    act.wait_ge(main_done, b + 1 + i)
                    act.activation(outs[:, b % NOUT, a:e], ps[:, bk, 0:e - a], ACT.Copy).then_inc(out_copied, 1)

            v_high(0)
            v_high(1)
            v_turned(0)
            v_turned(1)
            gate_exp(0)
            hgt_high(0)
            for b in range(1, NB):
                gate_exp(b)
                if b == 1:
                    v_high(2)
                out_copy(b - 1)
                if 1 < b < NB - 1:
                    v_high(b + 1)
                hgt_high(b)
                if b + 1 < NB:
                    v_turned(b + 1)
            out_copy(NB - 1)

        @block.vector
        def _(dve):
            chain = [0]

            def link(ins):
                chain[0] += 1
                ins.then_inc(dve_chain, 1)
                dve.wait_ge(dve_chain, chain[0])

            def lo_of(name):
                if name in NO_LOW:
                    return
                dve.wait_ge(high, HIGHS[name])
                src, dst, by = place(name)
                hi = dst[:, HI].bitcast(F32)
                if by == 1.0:
                    dve.tensor_tensor(dst[:, LO], src, hi, ALU.subtract).then_inc(low, 1)
                else:
                    dve.scalar_tensor_tensor(dst[:, LO], src, by, hi, ALU.mult, ALU.subtract).then_inc(low, 1)

            dve.wait_ge(ld_cb, 16)
            link(dve.tensor_reduce(tiny[:, 0:1], cb[:], AX.X, ALU.max))
            link(dve.tensor_reduce(tiny[:, 1:2], cb[:], AX.X, ALU.min))
            link(dve.tensor_scalar(tiny[:, 1:2], tiny[:, 1:2], -1.0, 1e-8, ALU.mult, ALU.max))
            link(dve.tensor_tensor(tiny[:, 0:1], tiny[:, 0:1], tiny[:, 1:2], ALU.max))
            link(dve.reciprocal(tiny[:, 2:3], tiny[:, 0:1]))
            link(dve.tensor_scalar(cbn[:], cb[:], tiny[:, 2:3], None, ALU.mult))
            link(dve.tensor_tensor(thr[:, 0:7], cbn[:, 0:7], cbn[:, 1:8], ALU.add))
            link(dve.tensor_scalar(thr[:, 0:7], thr[:, 0:7], 0.5, None, ALU.mult))
            link(dve.tensor_tensor(step[:, 0:7], cbn[:, 1:8], cbn[:, 0:7], ALU.subtract))
            dve.wait_ge(la_hi, 1)
            dve.tensor_tensor(la_s[:, LO], la[:], la_s[:, HI].bitcast(F32), ALU.subtract).then_inc(la_lo, 1)
            lo_of("lbt")
            link(dve.tensor_tensor(thr[:, 2:3], thr[:, 2:3], thr[:, 1:2], ALU.max))
            link(dve.tensor_tensor(thr[:, 2:3], thr[:, 2:3], thr[:, 3:4], ALU.min))
            link(dve.tensor_tensor(thr[:, 1:2], thr[:, 1:2], thr[:, 3:4], ALU.min))
            link(dve.tensor_tensor(thr[:, 0:1], thr[:, 0:1], thr[:, 1:2], ALU.min))
            link(dve.tensor_tensor(thr[:, 4:5], thr[:, 4:5], thr[:, 5:6], ALU.min))
            link(dve.tensor_tensor(thr[:, 4:5], thr[:, 4:5], thr[:, 3:4], ALU.max))
            link(dve.tensor_tensor(thr[:, 5:6], thr[:, 5:6], thr[:, 3:4], ALU.max))
            link(dve.tensor_tensor(thr[:, 6:7], thr[:, 6:7], thr[:, 5:6], ALU.max))
            for n in USES[AT["p3_0"]:AT["c0"]]:
                lo_of(n)
            dve.wait_ge(r2_hi, 1)
            dve.tensor_tensor(r2_s[:, LO], r2[:], r2_s[:, HI].bitcast(F32), ALU.subtract).then_inc(r2_lo, 1)
            lo_of("c0")
            lo_of("c1")
            dve.wait_ge(exped, 1)
            dve.reciprocal(rscale[:], scale[:]).then_inc(rs_ready, 1)
            dve.wait_ge(rs_ready, 1)
            for k in range(KT):
                if k % 2 == 0:
                    dve.wait_ge(ld_w0[k // 2], 16)
                dve.wait_ge(high, HIGHS[f"ld{k}"])
                dve.tensor_tensor(w0[:, k], w0[:, k], ld[:, k], ALU.add).then_inc(shifted, 1)

            def level(pair, s, par):
                i = 6 - s
                n = nrm[:, 2 * pair + par].rearrange("p k n -> p (k n)")
                a = acc[:, par].rearrange("p k n -> p (k n)")
                if s == 0:
                    dve.wait_ge(*((q_n, 2 * pair + par) if pair + par else (q_n0, 1)))
                    if pair:
                        dve.wait_ge(q_err, par + 1)
                    dve.tensor_scalar(a, n, thr[:, i:i + 1], step[:, i:i + 1], ALU.is_gt, ALU.mult)\
                        .then_inc(q_sum, 1)
                else:
                    dve.wait_ge(q_bias, 12 * pair + 2 * (s - 1) + par + 1)
                    b = bia[:, par].rearrange("p k n -> p (k n)")
                    dve.scalar_tensor_tensor(a, n, thr[:, i:i + 1], b, ALU.is_gt, ALU.mult).then_inc(q_sum, 1)

            def error_of(pair, par):
                g = 2 * pair + par
                dve.wait_ge(q_sum, 14 * pair + 12 + par + 1)
                dve.scalar_tensor_tensor(w0[:, :, g * P:(g + 1) * P], acc[:, par], cbn[:, 0:1], nrm[:, g],
                                         ALU.add, ALU.subtract).then_inc(q_err, 1)

            late = ["t2a", "t2b"]
            for pair in range(2):
                if pair == 0:
                    dve.wait_ge(shifted, KT)
                    dve.tensor_tensor(nrm[:, 0], w0[:, :, 0:P], rscale[:, :, 0:1].to_broadcast([P, KT, P]), ALU.mult)\
                        .then_inc(q_n0, 1)
                for s in range(6):
                    level(pair, s, 0)
                    level(pair, s, 1)
                    for n in late:
                        lo_of(n)
                    late = BESIDE[pair][s]
                level(pair, 6, 0)
                error_of(pair, 0)
                level(pair, 6, 1)
                for n in late:
                    lo_of(n)
                error_of(pair, 1)
                late = BESIDE[pair][6]
                if pair == 0:
                    lo_of(late[0])
                    late = late[1:]
            for n in late:
                lo_of(n)
            dve.wait_ge(q_err, G)
            link(dve.memset(vn[:].bitcast(F32), 0.0))
            dve.wait_ge(ld_lang, 16)
            dve.wait_ge(counted, 1)
            link(dve.tensor_copy(lang[:], lang_i[:]))
            link(dve.tensor_copy(iota[:], iota_i[:]))
            link(dve.tensor_tensor(lbias[:], iota[:, None, :].to_broadcast([P, NB, E]),
                                   lang[:, :, None].to_broadcast([P, NB, E]), ALU.is_equal))
            link(dve.tensor_scalar(lbias[:], lbias[:], LANG_BIAS, None, ALU.mult))
            for n in USES[AT["r02"]:]:
                lo_of(n)

            def v_low(b):
                dve.wait_ge(v_hi, b + 1)
                dve.tensor_tensor(vn[:, b % 2, LO_ROW:VW], ps[:, SMALL[b % 2], SW - V:SW],
                                  vn[:, b % 2, 0:V].bitcast(F32), ALU.subtract).then_inc(v_lo, 1)

            def hgt_low(b):
                dve.wait_ge(hgt_hi, b + 1)
                dve.tensor_tensor(hgt[:, LO], ps[:, HGT_BANK, 0:T], hgt[:, HI].bitcast(F32), ALU.subtract)\
                    .then_inc(hgt_lo, 1)

            def gates(b):
                small = ps[:, SMALL[b % 2], 0:NC]
                dve.wait_ge(z_small, b + 1)
                link(dve.tensor_tensor(lg[:], small[:, 0:E], lbias[:, b], ALU.add))
                link(dve.max(top[:], lg[:]))
                dve.tensor_tensor(gw[:, 0:1], top[:, 1:2], top[:, 0:1], ALU.subtract).then_inc(gap_ready, 1)
                link(dve.max_index(top_i[:], top[:], lg[:]))
                link(dve.tensor_copy(top_f[:], top_i[:]))
                dve.wait_ge(exp_done, b + 1)
                link(dve.tensor_scalar(gw[:, 2:3], gw[:, 1:2], 1.0, None, ALU.add))
                link(dve.reciprocal(gw[:, 3:4], gw[:, 2:3]))
                link(dve.tensor_tensor(gw[:, 4:5], gw[:, 1:2], gw[:, 3:4], ALU.mult))
                link(dve.tensor_scalar(gate[:, 0], iota[:], top_f[:, 0:1], gw[:, 3:4], ALU.is_equal, ALU.mult))
                link(dve.tensor_scalar(gate[:, 1], iota[:], top_f[:, 1:2], gw[:, 4:5], ALU.is_equal, ALU.mult))
                link(dve.tensor_tensor(gate[:, 2], gate[:, 0], gate[:, 1], ALU.add))
                if b >= 2:
                    dve.wait_ge(hgt_up, b - 1)
                dve.tensor_tensor(hg[:, b % 2].rearrange("p (e r) -> p e r", e=E),
                                  small[:, E:NC].rearrange("p (e r) -> p e r", e=E),
                                  gate[:, 2, :, None].to_broadcast([P, E, RE]), ALU.mult).then_inc(hg_ready, 1)

            v_low(0)
            v_low(1)
            for b in range(NB):
                gates(b)
                if 1 <= b < NB - 1:
                    v_low(b + 1)
                hgt_low(b)

        @block.tensor
        def _(pe):
            def use(name):
                if AT[name] >= 8:
                    before = USES[AT[name] - 8]
                    if before in NO_LOW:
                        pe.wait_ge(high, HIGHS[before])
                    else:
                        pe.wait_ge(low, LOWS[before])

            def split(name):
                pe.wait_ge(low, LOWS[name])

            def product(dst, terms, first=True, last=True):
                n = 0
                for lhs, rhs in terms:
                    for a, b in PASSES:
                        mm = pe.matmul(dst, lhs(a), rhs(b), start=(first and n == 0),
                                       stop=(last and n == 3 * len(terms) - 1))
                        n += 1
                return mm

            pe.wait_ge(made, 2)
            for k in range(WARM_UPS):
                pe.transpose(bank("c1")[:, 0:P], ident[:], ident[:])
            use("lbt")
            pe.wait_ge(ld_lb, 16)
            for k in range(KT):
                mm = pe.transpose(bank("lbt")[0:RL0, k * P:(k + 1) * P], lb[:, k], ident[:])
            mm.then_inc(filled, 1)
            for k in range(WARM_AGAIN):
                pe.transpose(bank("c1")[:, 0:P], ident[:], ident[:])
            for half in range(2):
                pe.wait_ge(ld_w3[half], 16)
                for m in range(KT):
                    use(f"p3_{m}")
                    for k in sorted((2 * half, 2 * half + 1), key=lambda k: k == m):
                        if k == m:
                            pe.wait_ge(eye3, k + 1)
                        mm = pe.transpose(bank(f"p3_{m}")[:, k * P:(k + 1) * P], w3[:, k, m * P:(m + 1) * P], ident[:])
                    if half:
                        mm.then_inc(filled, 1)
            pe.wait_ge(ld_wr, 16)
            pe.wait_ge(ld_a3, 16)
            for j in range(2):
                use(f"c{j}")
                for i in range(2):
                    k = 2 * j + i
                    pe.transpose(bank(f"c{j}")[:, i * NC:i * NC + E], wr[:, k * P:(k + 1) * P], ident[0:E, 0:E])
                    mm = pe.transpose(bank(f"c{j}")[:, i * NC + E:(i + 1) * NC], a3[:, k * P:(k + 1) * P], ident[:])
                mm.then_inc(filled, 1)

            def w2_cols(m, i):
                return lambda s: pc[:, s, m, QW + i * P:QW + (i + 1) * P]

            def p3c(m, h):
                return lambda s: pc[:, s, m, h * QP:(h + 1) * QP]

            def qcv(m, a, b):
                return lambda s: qc[:, s, m, a:b]

            def ld_block(k):
                use(f"ld{k}")
                product(bank(f"ld{k}"), [(lambda s: lbt_s[:, s, k * P:(k + 1) * P], lambda s: la_s[:, s])])\
                    .then_inc(filled, 1)

            split("lbt")
            pe.wait_ge(la_lo, 1)
            for k in range(KT):
                ld_block(k)
            pe.wait_ge(r2_lo, 1)
            for h in range(2):
                name = "t2" + "ab"[h]
                use(name)
                split(("p3_3", "c1")[h])
                product(bank(name)[0:RB, 0:QP], [(lambda s, m=m: r2_s[:, s, m], p3c(m, h)) for m in range(KT)])\
                    .then_inc(filled, 1)

            def qc_block(i, h):
                name = f"qc{i}" + "ab"[h]
                use(name)
                for m in range(KT):
                    if i == h == 0:
                        pe.wait_ge(w2_low, m + 1)
                    mm = product(bank(name)[:, 0:QP], [(w2_cols(m, i), p3c(m, h))], m == 0, m == KT - 1)
                mm.then_inc(filled, 1)

            for i in range(KT):
                qc_block(i, 0)
                qc_block(i, 1)
            use("al")
            pe.wait_ge(l2_lo, 1)
            pe.wait_ge(a1_lo, 1)
            product(bank("al")[:, 0:NB * RB], [(lambda s, k=k: a1_s[:, s, k], lambda s, k=k: l2_cols[:, s, k])
                                               for k in range(KT)]).then_inc(filled, 1)
            use("b1t")
            pe.wait_ge(ld_b1, 16 * NB)
            for k in range(KT):
                mm = pe.transpose(bank("b1t")[:, k * P:(k + 1) * P], b1[:, k * P:(k + 1) * P], ident[:])
            mm.then_inc(filled, 1)
            use("alt")
            pe.wait_ge(high, HIGHS["al"])
            for b in range(NB):
                mm = pe.matmul(bank("alt")[0:RB, b * RA:(b + 1) * RA], al[:, b], ident[:, b * RA:(b + 1) * RA],
                               start=True, stop=True)
            mm.then_inc(filled, 1)
            for h in range(2):
                a, b = h * QP, (h + 1) * QP
                use("t1" + "ab"[h])
                for m in range(KT):
                    split(f"qc{m}" + "ab"[h])
                    product(bank("t1" + "ab"[h])[:, 0:QP], [(lambda s, m=m: a1_s[:, s, m], qcv(m, a, b))],
                            m == 0, False)
            split("t2b")
            split("alt")
            for h in range(2):
                a, b = h * QP, (h + 1) * QP
                product(bank("t1" + "ab"[h])[:, 0:QP],
                        [(lambda s: al_s[:, s], lambda s, a=a, b=b: t2[:, s, a:b])],
                        first=False).then_inc(filled, 1)

            def r_block(g):
                pe.wait_ge(w0_lo, g + 1)
                for c in range(3):
                    use(f"r{g}{c}")
                    if g == 0 and c == 1:
                        split("b1t")
                    product(bank(f"r{g}{c}")[:, 0:RP],
                            [(lambda s, m=m: w0_s[:, s, m, g * P:(g + 1) * P], qcv(m, c * RP, (c + 1) * RP))
                             for m in range(KT)]).then_inc(filled, 1)

            r_block(0)
            r_block(1)
            for b in range(NB):
                use(f"x{b}")
                if b % 4 == 0:
                    pe.wait_ge(ld_x[b // 4], 16)
                src = (x_a, x_b)[b // 4]
                for k in range(KT):
                    mm = pe.transpose(bank(f"x{b}")[:, k * P:(k + 1) * P], src[:, b % 4, k * P:(k + 1) * P], ident[:])
                mm.then_inc(filled, 1)
            use("b3t")
            pe.wait_ge(ld_b3, 16 * KT)
            for k in range(KT):
                mm = pe.transpose(bank("b3t")[:, k * P:(k + 1) * P], b3[:, k].rearrange("p e r -> p (e r)"), ident[:])
            mm.then_inc(filled, 1)
            r_block(2)
            r_block(3)

            row = 2 * KT * XW

            def small_cols(b, k, s):
                base = pc[:, s, k, D:QW]
                return bass.AP(base.tensor, base.offset, [[row, P], [(b + 1) * V, 2], [1, NC]])

            def small(b, ks):
                if b >= 2 and 0 in ks:
                    pe.wait_ge(hg_ready, b - 1)
                for k in ks:
                    for n, (u, w) in enumerate(PASSES):
                        mm = pe.matmul(ps[:, SMALL[b % 2], 0:SW], xt[:, u, b, k], small_cols(b, k, w),
                                       start=(k == 0 and n == 0), stop=(k == KT - 1 and n == 2))
                if KT - 1 in ks:
                    mm.then_inc(small_done, 1)

            def main(b, ks):
                if b >= 3 and 0 in ks:
                    pe.wait_ge(out_copied, b - 3 + len(main_parts(b)))
                for bk, a, e in main_parts(b):
                    for k in ks:
                        for n, (u, w) in enumerate(PASSES):
                            pe.matmul(ps[:, bk, 0:e - a], xt[:, u, b, k], pc[:, w, k, a:e],
                                      start=(k == 0 and n == 0), stop=False, skip_group_check=True)

            def turn_v(b):
                pe.wait_ge(v_lo, b + 1)
                if b >= 1:
                    pe.wait_ge(vt_copied, b)
                pe.transpose(ps[0:VW, VT_BANK, 0:T].bitcast(F32), vn[:, b % 2, 0:VW].bitcast(F32), ident[:])\
                    .then_inc(vt_up, 1)

            def add_v(b, dst, a, e, stop):
                s = b % NS
                pe.matmul(dst, vt[0:VW, b % 2], s_hi[:, s, a:e], start=False, stop=False, skip_group_check=True)
                return pe.matmul(dst, vt[0:V, b % 2], s_lo[:, s, a:e], start=False, stop=stop,
                                 skip_group_check=True)

            def add_v_small(b):
                pe.wait_ge(vt_copied, b + 1)
                pe.wait_ge(s_loaded[b % NS], 48 * (b // NS + 2))
                add_v(b, ps[:, SMALL[b % 2], 0:NC], D, QW, True).then_inc(z_small, 1)

            def add_v_main(b):
                for bk, a, e in main_parts(b):
                    mm = add_v(b, ps[:, bk, 0:e - a], a, e, False)
                mm.then_inc(z_main, 1)

            def turn_hg(b):
                pe.wait_ge(hg_ready, b + 1)
                if b >= 1:
                    pe.wait_ge(hgt_lo, b)
                pe.transpose(ps[:, HGT_BANK, 0:T], hg[:, b % 2], ident[:]).then_inc(hgt_up, 1)

            def add_experts(b):
                pe.wait_ge(hgt_lo, b + 1)
                for bk, a, e in main_parts(b):
                    for n, (u, w) in enumerate(PASSES):
                        mm = pe.matmul(ps[:, bk, 0:e - a], hgt[:, u], b3t[:, w, a:e], start=False, stop=(n == 2),
                                       skip_group_check=True)
                    mm.then_inc(main_done, 1)

            split(f"r{G - 2}2")
            small(0, range(KT - 1))
            main(0, range(KT - 1))
            split(f"r{G - 1}2")
            small(0, [KT - 1])
            small(1, range(KT))
            turn_v(0)
            main(0, [KT - 1])
            add_v_small(0)
            turn_v(1)
            main(1, [0])
            add_v_main(0)
            add_v_small(1)
            main(1, [1, 2, 3])
            turn_hg(0)
            add_v_main(1)
            small(2, range(KT))
            add_experts(0)
            for b in range(2, NB - 2):
                if b > 2:
                    small(b, range(KT))
                main(b, [0, 1])
                turn_hg(b - 1)
                turn_v(b)
                main(b, [2])
                add_v_small(b)
                add_experts(b - 1)
                main(b, [3])
                add_v_main(b)
            b, z = NB - 2, NB - 1
            small(b, range(KT))
            main(b, [0])
            turn_hg(b - 1)
            turn_v(b)
            main(b, [1])
            add_v_small(b)
            add_experts(b - 1)
            small(z, range(KT))
            main(b, [2])
            turn_hg(b)
            turn_v(z)
            main(b, [3])
            add_v_small(z)
            add_v_main(b)
            add_experts(b)
            main(z, [0, 1, 2])
            turn_hg(z)
            main(z, [3])
            add_v_main(z)
            add_experts(z)


_INS = ["x", "condB_codebook", "itok_B_3_7", "itok_B_0_2", "itok_B_0_7", "L0_cond_weight", "L0_cond_scale_log",
        "L0_cond_lora_A", "L0_cond_lora_B", "L1_cond_A", "L1_cond_B", "L2_cond_W", "L2_cond_lora_A",
        "L2_cond_lora_B_w", "L3_cond_W", "L3_cond_Wr", "L3_cond_A", "L3_cond_B"]


def kernel(**inputs):
    import numpy as np
    import concourse.bacc as bacc
    from concourse.bass_utils import run_bass_kernel_spmd

    nc = bacc.Bacc("TRN2", target_bir_lowering=False, num_devices=1)
    arrays, args = {}, []
    for name in _INS:
        a = np.ascontiguousarray(inputs[name])
        arrays[f"in_{name}"] = a
        args.append(nc.dram_tensor(f"in_{name}", a.shape, mybir.dt.from_np(a.dtype), kind="ExternalInput").ap())
    out = nc.dram_tensor("out_dram", inputs["x"].shape, F32, kind="ExternalOutput").ap()
    layer_chain(nc, *args, out)
    r = run_bass_kernel_spmd(nc, [arrays], core_ids=[0])
    return r.results[0]["out_dram"]
```
